# Optimizing a Trainium2 kernel written in Bass

```python
import numpy as np
import jax
import jax.numpy as jnp

def _softmax(x, axis=-1):
    return jax.nn.softmax(x, axis=axis)

def _gelu(x):
    return jax.nn.gelu(x, approximate=True)

def _silu(x):
    return jax.nn.silu(x)

def _sigmoid(x):
    return jax.nn.sigmoid(x)

def _layernorm(x, axis=-1, eps=1e-05):
    m = jnp.mean(x, axis=axis, keepdims=True)
    v = jnp.var(x, axis=axis, keepdims=True)
    return (x - m) / jnp.sqrt(v + eps)

def _scatter_add(tgt, idx, src, axis=0):
    return tgt.at[idx].add(src)

def _segment_sum(src, seg, n):
    return jax.ops.segment_sum(src, seg, n)
kernel_name = 'mk_decoder_postln_d2_seqx_r8_eeb5fe'

def setup_inputs(seed: int=0):
    np.random.seed(seed)
    _w = jnp.asarray

    def _rec_inputs():
        import jax
        import jax.numpy as jnp
        _rk = jax.random.key(seed)
        x = -0.0002928 + 1 * jax.random.normal(jax.random.fold_in(_rk, 1), (16, 64, 128), jnp.float32)
        _lenS = 64 - jax.random.randint(jax.random.fold_in(_rk, 7), (16,), 0, max(1, 64 // 4) + 1, jnp.int32)
        _lenS2 = 64 - jax.random.randint(jax.random.fold_in(_rk, 8), (16,), 0, max(1, 64 // 4) + 1, jnp.int32)
        _ctx_2048P = jax.random.normal(jax.random.fold_in(_rk, 11), (16, 16, 256), jnp.float32)
        _ctx_2048c = jax.random.dirichlet(jax.random.fold_in(_rk, 511), 0.3 * jnp.ones((16,), jnp.float32), (16, 64))
        _ctx_2048t = jnp.einsum('bsk,bkd->bsd', _ctx_2048c, _ctx_2048P)
        _ctx_2048t = _ctx_2048t * jax.lax.rsqrt(jnp.mean(jnp.square(_ctx_2048t)) + 1e-12) * 0.953939
        ctx_2048 = -0.000514642 + 1.00011 * (_ctx_2048t + 0.3 * jax.random.normal(jax.random.fold_in(_rk, 611), (16, 64, 256), jnp.float32))
        _validS = jnp.arange(64)[None, :] < _lenS[:, None]
        _validS2 = jnp.arange(64)[None, :] < _lenS2[:, None]
        _causal = jnp.tril(jnp.ones((64, 64), dtype=bool))
        mask_BxS2_ik0 = jnp.where(jnp.broadcast_to(_validS2[:, :], (16, 64)), 0, 1).astype(jnp.int32)
        return (x, ctx_2048, mask_BxS2_ik0)
    x, ctx_2048, mask_BxS2_ik0 = _rec_inputs()

    def _L0_attn_setup():
        import jax, jax.numpy as jnp
        import numpy as np
        D_MODEL = 128
        N_HEADS = 16
        D_K = D_MODEL // N_HEADS

        def _rope_cache(T, dtype):
            half = D_K // 2
            freq = 1.0 / 10000.0 ** (2.0 * jnp.arange(half, dtype=dtype) / D_K)
            angles = jnp.arange(T, dtype=dtype)[:, None] * freq[None, :]
            return (jnp.cos(angles), jnp.sin(angles))

        def _apply_rope(x, cos, sin):
            half = x.shape[-1] // 2
            x1, x2 = (x[..., :half], x[..., half:])
            return jnp.concatenate([x1 * cos - x2 * sin, x1 * sin + x2 * cos], axis=-1)
        key = jax.random.key(seed)
        ks = jax.random.split(key, 9)
        s = 0.02
        return {'x': jax.random.normal(ks[0], (4, 256, D_MODEL), dtype=jnp.float32), 'WQ_w': jax.random.normal(ks[1], (D_MODEL, D_MODEL), dtype=jnp.float32) * s, 'WQ_b': jax.random.normal(ks[2], (D_MODEL,), dtype=jnp.float32) * s, 'WK_w': jax.random.normal(ks[3], (D_MODEL, D_MODEL), dtype=jnp.float32) * s, 'WK_b': jax.random.normal(ks[4], (D_MODEL,), dtype=jnp.float32) * s, 'WV_w': jax.random.normal(ks[5], (D_MODEL, D_MODEL), dtype=jnp.float32) * s, 'WV_b': jax.random.normal(ks[6], (D_MODEL,), dtype=jnp.float32) * s, 'Wo_w': jax.random.normal(ks[7], (D_MODEL, D_MODEL), dtype=jnp.float32) * s, 'Wo_b': jax.random.normal(ks[8], (D_MODEL,), dtype=jnp.float32) * s}
    _L0_attn_all = _L0_attn_setup()
    _L0_attn_in = {k: v for k, v in _L0_attn_all.items() if k in ('WQ_w', 'WQ_b', 'WK_w', 'WK_b', 'WV_w', 'WV_b', 'Wo_w', 'Wo_b')}
    del _L0_attn_all

    def _L0_xattn_setup():
        import jax, jax.numpy as jnp
        import numpy as np
        NUM_HEADS = 16
        key = jax.random.key(seed)
        ks = jax.random.split(key, 5)
        dim = 128
        B, N, N_c = (4, 128, 32)
        x = jax.random.normal(ks[0], (B, N, dim), dtype=jnp.float32)
        context = jax.random.normal(ks[1], (B, N_c, 2 * dim), dtype=jnp.float32)
        w_qkv = jax.random.normal(ks[2], (3 * dim, dim), dtype=jnp.float32) * 0.02
        w_proj = jax.random.normal(ks[3], (dim, dim), dtype=jnp.float32) * 0.02
        b_proj = jax.random.normal(ks[4], (dim,), dtype=jnp.float32) * 0.02
        return {'x': x, 'context': context, 'w_qkv': w_qkv, 'w_proj': w_proj, 'b_proj': b_proj}
    _L0_xattn_all = _L0_xattn_setup()
    _L0_xattn_in = {k: v for k, v in _L0_xattn_all.items() if k in ('w_qkv', 'w_proj', 'b_proj')}
    del _L0_xattn_all

    def _L0_ffn_setup():
        import jax, jax.numpy as jnp
        import numpy as np
        NUM_EXPERTS = 8
        TOP_K = 2
        MOE_DIM = 256

        def _moe_forward(x, moe_router, moe_w13, moe_w2):
            b, s, d = x.shape
            x_flat = x.reshape(b * s, d)
            router_logits = jnp.einsum('td,de->te', x_flat, moe_router)
            topk_logits, topk_idx = jax.lax.top_k(router_logits, TOP_K)
            topk_weights = jax.nn.softmax(topk_logits, axis=-1).astype(x.dtype)
            tokens = x_flat.shape[0]
            expert_ids = topk_idx.reshape(tokens * TOP_K)
            dispatch_weights = topk_weights.reshape(tokens * TOP_K)
            sort_idx = jnp.argsort(expert_ids, axis=0)
            token_ids = jnp.arange(tokens * TOP_K, dtype=jnp.int32) // TOP_K
            token_ids_sort = token_ids[sort_idx]
            x_sort = x_flat[token_ids_sort]
            w_sort = dispatch_weights[sort_idx].astype(x_flat.dtype)
            group_sizes = jnp.bincount(expert_ids, length=NUM_EXPERTS).astype(jnp.int32)
            w13_out = jax.lax.ragged_dot(x_sort, moe_w13, group_sizes)
            gate, up = jnp.split(w13_out, [MOE_DIM], axis=-1)
            hidden = jax.nn.silu(gate) * up
            out_dispatch = jax.lax.ragged_dot(hidden, moe_w2, group_sizes)
            out_flat = jnp.zeros_like(x_flat).at[token_ids_sort].add(out_dispatch * w_sort[:, None], mode='drop')
            return out_flat.reshape(b, s, d)
        key = jax.random.key(seed)
        k1, k2, k3, k4 = jax.random.split(key, 4)
        B, S, D = (4, 256, 128)
        x = jax.random.normal(k1, (B, S, D), dtype=jnp.float32)
        moe_router = jax.random.normal(k2, (D, NUM_EXPERTS), dtype=jnp.float32) * 0.02
        moe_w13 = jax.random.normal(k3, (NUM_EXPERTS, D, 2 * MOE_DIM), dtype=jnp.float32) * 0.02
        moe_w2 = jax.random.normal(k4, (NUM_EXPERTS, MOE_DIM, D), dtype=jnp.float32) * 0.02
        return {'x': x, 'moe_router': moe_router, 'moe_w13': moe_w13, 'moe_w2': moe_w2}
    _L0_ffn_all = _L0_ffn_setup()
    _L0_ffn_in = {k: v for k, v in _L0_ffn_all.items() if k in ('moe_router', 'moe_w13', 'moe_w2')}
    del _L0_ffn_all

    def _L1_attn_setup():
        import jax, jax.numpy as jnp
        import numpy as np
        D_MODEL = 128
        D_STATE = 16
        D_CONV = 4
        EXPAND = 2
        DT_RANK = 64
        D_INNER = EXPAND * D_MODEL
        B = 2
        L = 256
        key = jax.random.key(seed)
        ks = jax.random.split(key, 8)
        g = lambda i, shape, scale: jax.random.normal(ks[i], shape, dtype=jnp.float32) * scale
        return {'hidden_states': jax.random.normal(ks[0], (B, L, D_MODEL), dtype=jnp.float32), 'in_proj_w': g(1, (2 * D_INNER, D_MODEL), 0.02), 'conv_w': g(2, (D_INNER, 1, D_CONV), 0.2), 'conv_b': jnp.zeros((D_INNER,), jnp.float32), 'x_proj_w': g(3, (DT_RANK + 2 * D_STATE, D_INNER), 0.02), 'dt_head_w': g(4, (D_INNER, DT_RANK), 0.1), 'dt_head_b': g(5, (D_INNER,), 0.1), 'out_proj_w': g(6, (D_MODEL, D_INNER), 0.02), 'D': jnp.ones((D_INNER,), jnp.float32)}
    _L1_attn_all = _L1_attn_setup()
    _L1_attn_in = {k: v for k, v in _L1_attn_all.items() if k in ('in_proj_w', 'conv_w', 'conv_b', 'x_proj_w', 'dt_head_w', 'dt_head_b', 'out_proj_w', 'D')}
    del _L1_attn_all

    def _L1_xattn_setup():
        import jax, jax.numpy as jnp
        import numpy as np
        UNITS = 128
        NUM_HEADS = 8

        def _split_heads(x, n):
            B, S, D = x.shape
            return x.reshape(B, S, n, D // n).transpose(0, 2, 1, 3)
        key = jax.random.key(seed)
        k1, k2, k3 = jax.random.split(key, 3)
        B, S = (8, 128)
        memory = jax.random.normal(k1, (B, S, 2 * UNITS), dtype=jnp.float32)
        query = jax.random.normal(k2, (B, S, UNITS), dtype=jnp.float32)
        seq_mask = jax.random.randint(k3, (B, S), 0, 2, dtype=jnp.int32)
        b = jnp.zeros((1,), dtype=jnp.float32)
        return {'memory': memory, 'query': query, 'seq_mask': seq_mask, 'b': b}
    _L1_xattn_all = _L1_xattn_setup()
    _L1_xattn_in = {k: v for k, v in _L1_xattn_all.items() if k in ('b',)}
    del _L1_xattn_all

    def _L1_ffn_setup():
        import jax, jax.numpy as jnp
        import numpy as np
        B, N, D, H, E = (4, 128, 128, 16, 8)
        DK = D // H
        HID = 4 * D
        EPS = 1e-05

        def _layernorm(x, w, b):
            m = jnp.mean(x, axis=-1, keepdims=True)
            v = jnp.mean(jnp.square(x - m), axis=-1, keepdims=True)
            return (x - m) * jax.lax.rsqrt(v + EPS) * w + b

        def _msa(x, w_qkv, w_proj):
            b, n, d = x.shape
            qkv = (x @ w_qkv).reshape(b, n, 3, H, DK)
            q = qkv[:, :, 0].transpose(0, 2, 1, 3)
            k = qkv[:, :, 1].transpose(0, 2, 1, 3)
            v = qkv[:, :, 2].transpose(0, 2, 1, 3)
            attn = jnp.einsum('bhnd,bhmd->bhnm', q, k) * (1.0 / np.sqrt(DK))
            attn = jax.nn.softmax(attn, axis=-1)
            y = jnp.einsum('bhnm,bhmd->bhnd', attn, v)
            y = y.transpose(0, 2, 1, 3).reshape(b, n, d)
            return y @ w_proj

        def _moe_mlp(x, gate_w, gate_b, w1, w2):
            b, n, d = x.shape
            xf = x.reshape(b * n, d)
            logits = xf @ gate_w + gate_b
            one_hot = jax.nn.one_hot(jnp.argmax(logits, axis=-1), E, dtype=xf.dtype)
            h = jax.nn.gelu(jnp.einsum('td,edh->teh', xf, w1), approximate=True)
            y = jnp.einsum('teh,ehd->ted', h, w2)
            out = jnp.einsum('te,ted->td', one_hot, y)
            return out.reshape(b, n, d)
        key = jax.random.key(seed)
        ks = jax.random.split(key, 8)
        s = 0.02
        return {'x': jax.random.normal(ks[0], (B, N, D), jnp.float32), 'ln1_w': jnp.ones((D,), jnp.float32), 'ln1_b': jnp.zeros((D,), jnp.float32), 'w_qkv': jax.random.normal(ks[1], (D, 3 * D), jnp.float32) * s, 'w_proj': jax.random.normal(ks[2], (D, D), jnp.float32) * s, 'ln2_w': jnp.ones((D,), jnp.float32), 'ln2_b': jnp.zeros((D,), jnp.float32), 'gate_w': jax.random.normal(ks[3], (D, E), jnp.float32) * s, 'gate_b': jnp.zeros((E,), jnp.float32), 'w1': jax.random.normal(ks[4], (E, D, HID), jnp.float32) * s, 'w2': jax.random.normal(ks[5], (E, HID, D), jnp.float32) * s}
    _L1_ffn_all = _L1_ffn_setup()
    _L1_ffn_in = {k: v for k, v in _L1_ffn_all.items() if k in ('ln1_w', 'ln1_b', 'w_qkv', 'w_proj', 'ln2_w', 'ln2_b', 'gate_w', 'gate_b', 'w1', 'w2')}
    del _L1_ffn_all
    return {'x': x, 'ctx_2048': ctx_2048, 'mask_BxS2_ik0': mask_BxS2_ik0, 'L0_attn_WQ_w': _L0_attn_in['WQ_w'], 'L0_attn_WQ_b': _L0_attn_in['WQ_b'], 'L0_attn_WK_w': _L0_attn_in['WK_w'], 'L0_attn_WK_b': _L0_attn_in['WK_b'], 'L0_attn_WV_w': _L0_attn_in['WV_w'], 'L0_attn_WV_b': _L0_attn_in['WV_b'], 'L0_attn_Wo_w': _L0_attn_in['Wo_w'], 'L0_attn_Wo_b': _L0_attn_in['Wo_b'], 'L0_xattn_w_qkv': _L0_xattn_in['w_qkv'], 'L0_xattn_w_proj': _L0_xattn_in['w_proj'], 'L0_xattn_b_proj': _L0_xattn_in['b_proj'], 'L0_ffn_moe_router': _L0_ffn_in['moe_router'], 'L0_ffn_moe_w13': _L0_ffn_in['moe_w13'], 'L0_ffn_moe_w2': _L0_ffn_in['moe_w2'], 'L1_attn_in_proj_w': _L1_attn_in['in_proj_w'], 'L1_attn_conv_w': _L1_attn_in['conv_w'], 'L1_attn_conv_b': _L1_attn_in['conv_b'], 'L1_attn_x_proj_w': _L1_attn_in['x_proj_w'], 'L1_attn_dt_head_w': _L1_attn_in['dt_head_w'], 'L1_attn_dt_head_b': _L1_attn_in['dt_head_b'], 'L1_attn_out_proj_w': _L1_attn_in['out_proj_w'], 'L1_attn_D': _L1_attn_in['D'], 'L1_xattn_b': _L1_xattn_in['b'], 'L1_ffn_ln1_w': _L1_ffn_in['ln1_w'], 'L1_ffn_ln1_b': _L1_ffn_in['ln1_b'], 'L1_ffn_w_qkv': _L1_ffn_in['w_qkv'], 'L1_ffn_w_proj': _L1_ffn_in['w_proj'], 'L1_ffn_ln2_w': _L1_ffn_in['ln2_w'], 'L1_ffn_ln2_b': _L1_ffn_in['ln2_b'], 'L1_ffn_gate_w': _L1_ffn_in['gate_w'], 'L1_ffn_gate_b': _L1_ffn_in['gate_b'], 'L1_ffn_w1': _L1_ffn_in['w1'], 'L1_ffn_w2': _L1_ffn_in['w2']}

def reference(x, ctx_2048, mask_BxS2_ik0, L0_attn_WQ_w, L0_attn_WQ_b, L0_attn_WK_w, L0_attn_WK_b, L0_attn_WV_w, L0_attn_WV_b, L0_attn_Wo_w, L0_attn_Wo_b, L0_xattn_w_qkv, L0_xattn_w_proj, L0_xattn_b_proj, L0_ffn_moe_router, L0_ffn_moe_w13, L0_ffn_moe_w2, L1_attn_in_proj_w, L1_attn_conv_w, L1_attn_conv_b, L1_attn_x_proj_w, L1_attn_dt_head_w, L1_attn_dt_head_b, L1_attn_out_proj_w, L1_attn_D, L1_xattn_b, L1_ffn_ln1_w, L1_ffn_ln1_b, L1_ffn_w_qkv, L1_ffn_w_proj, L1_ffn_ln2_w, L1_ffn_ln2_b, L1_ffn_gate_w, L1_ffn_gate_b, L1_ffn_w1, L1_ffn_w2):
    import jax
    import jax.numpy as jnp

    def _L0_attn_ref(x, WQ_w, WQ_b, WK_w, WK_b, WV_w, WV_b, Wo_w, Wo_b):
        import jax, jax.numpy as jnp
        import numpy as np
        D_MODEL = 128
        N_HEADS = 16
        D_K = D_MODEL // N_HEADS

        def _rope_cache(T, dtype):
            half = D_K // 2
            freq = 1.0 / 10000.0 ** (2.0 * jnp.arange(half, dtype=dtype) / D_K)
            angles = jnp.arange(T, dtype=dtype)[:, None] * freq[None, :]
            return (jnp.cos(angles), jnp.sin(angles))

        def _apply_rope(x, cos, sin):
            half = x.shape[-1] // 2
            x1, x2 = (x[..., :half], x[..., half:])
            return jnp.concatenate([x1 * cos - x2 * sin, x1 * sin + x2 * cos], axis=-1)
        B, T, D = x.shape

        def proj(w, b):
            y = jnp.einsum('btd,ed->bte', x, w) + b
            return y.reshape(B, T, N_HEADS, D_K).transpose(0, 2, 1, 3)
        q = proj(WQ_w, WQ_b)
        k = proj(WK_w, WK_b)
        v = proj(WV_w, WV_b)
        cos, sin = _rope_cache(T, x.dtype)
        q = _apply_rope(q, cos, sin)
        k = _apply_rope(k, cos, sin)
        scores = jnp.einsum('bhqd,bhkd->bhqk', q, k) / jnp.sqrt(jnp.asarray(D_K, x.dtype))
        causal = jnp.tril(jnp.ones((T, T), dtype=bool))
        scores = jnp.where(causal[None, None, :, :], scores, -jnp.inf)
        attn = jax.nn.softmax(scores, axis=-1)
        out = jnp.einsum('bhqk,bhkd->bhqd', attn, v)
        out = out.transpose(0, 2, 1, 3).reshape(B, T, D)
        return jnp.einsum('btd,ed->bte', out, Wo_w) + Wo_b

    def _L0_xattn_ref(x, context, w_qkv, w_proj, b_proj):
        import jax, jax.numpy as jnp
        import numpy as np
        NUM_HEADS = 16
        B, N, C = x.shape
        H = NUM_HEADS
        D = C // H
        scale = D ** (-0.5)
        qkv = (x @ w_qkv.T).reshape(B, N, 3, H, D).transpose(2, 0, 3, 1, 4)
        q, k, v = (qkv[0], qkv[1], qkv[2])
        N_c = context.shape[1]
        kv = context.reshape(B, N_c, 2, H, D).transpose(2, 0, 3, 1, 4)
        extra_k, extra_v = (kv[0], kv[1])
        k = jnp.concatenate([extra_k, k], axis=2)
        v = jnp.concatenate([extra_v, v], axis=2)
        dtype = q.dtype
        attn = jnp.einsum('bhnd,bhmd->bhnm', q * scale, k).astype(jnp.float32)
        attn = jax.nn.softmax(attn, axis=-1).astype(dtype)
        out = jnp.einsum('bhnm,bhmd->bhnd', attn, v)
        out = out.transpose(0, 2, 1, 3).reshape(B, N, C)
        return out @ w_proj.T + b_proj

    def _L0_ffn_ref(x, moe_router, moe_w13, moe_w2):
        import jax, jax.numpy as jnp
        import numpy as np
        NUM_EXPERTS = 8
        TOP_K = 2
        MOE_DIM = 256

        def _moe_forward(x, moe_router, moe_w13, moe_w2):
            b, s, d = x.shape
            x_flat = x.reshape(b * s, d)
            router_logits = jnp.einsum('td,de->te', x_flat, moe_router)
            topk_logits, topk_idx = jax.lax.top_k(router_logits, TOP_K)
            topk_weights = jax.nn.softmax(topk_logits, axis=-1).astype(x.dtype)
            tokens = x_flat.shape[0]
            expert_ids = topk_idx.reshape(tokens * TOP_K)
            dispatch_weights = topk_weights.reshape(tokens * TOP_K)
            sort_idx = jnp.argsort(expert_ids, axis=0)
            token_ids = jnp.arange(tokens * TOP_K, dtype=jnp.int32) // TOP_K
            token_ids_sort = token_ids[sort_idx]
            x_sort = x_flat[token_ids_sort]
            w_sort = dispatch_weights[sort_idx].astype(x_flat.dtype)
            group_sizes = jnp.bincount(expert_ids, length=NUM_EXPERTS).astype(jnp.int32)
            w13_out = jax.lax.ragged_dot(x_sort, moe_w13, group_sizes)
            gate, up = jnp.split(w13_out, [MOE_DIM], axis=-1)
            hidden = jax.nn.silu(gate) * up
            out_dispatch = jax.lax.ragged_dot(hidden, moe_w2, group_sizes)
            out_flat = jnp.zeros_like(x_flat).at[token_ids_sort].add(out_dispatch * w_sort[:, None], mode='drop')
            return out_flat.reshape(b, s, d)
        return _moe_forward(x, moe_router, moe_w13, moe_w2)

    def _L1_attn_ref(hidden_states, in_proj_w, conv_w, conv_b, x_proj_w, dt_head_w, dt_head_b, out_proj_w, D):
        import jax, jax.numpy as jnp
        import numpy as np
        D_MODEL = 128
        D_STATE = 16
        D_CONV = 4
        EXPAND = 2
        DT_RANK = 64
        D_INNER = EXPAND * D_MODEL
        B = 2
        L = 256
        Bz, Lz, _ = hidden_states.shape
        xz = hidden_states @ in_proj_w.T
        x, z = jnp.split(xz, 2, axis=-1)
        xc = jnp.transpose(x, (0, 2, 1))
        xc = jax.lax.conv_general_dilated(xc, conv_w, window_strides=(1,), padding=[(D_CONV - 1, 0)], dimension_numbers=('NCH', 'OIH', 'NCH'), feature_group_count=D_INNER) + conv_b[None, :, None]
        x = jax.nn.silu(jnp.transpose(xc, (0, 2, 1)))
        x_dbl = x @ x_proj_w.T
        dt, k, q = jnp.split(x_dbl, [DT_RANK, DT_RANK + D_STATE], axis=-1)
        dt = dt @ dt_head_w.T

        def step(state, inp):
            x_t, dt_t, k_t, q_t = inp
            dtv = jax.nn.sigmoid(dt_t + dt_head_b)
            dtv = dtv / (1.0 + dtv * jnp.sum(k_t * k_t, axis=-1, keepdims=True))
            kk = k_t * k_t
            state = state * (1.0 - dtv[..., None] * kk[:, None, :]) + (x_t * dtv)[..., None] * k_t[:, None, :]
            y_t = jnp.einsum('bdn,bn->bd', state, q_t)
            return (state, y_t)
        init = jnp.zeros((Bz, D_INNER, D_STATE), hidden_states.dtype)
        xs = (jnp.transpose(x, (1, 0, 2)), jnp.transpose(dt, (1, 0, 2)), jnp.transpose(k, (1, 0, 2)), jnp.transpose(q, (1, 0, 2)))
        _, ys = jax.lax.scan(step, init, xs)
        y = jnp.transpose(ys, (1, 0, 2)) + D * x
        y = y * jax.nn.silu(z)
        out = y @ out_proj_w.T
        return out

    def _L1_xattn_ref(memory, query, seq_mask, b):
        import jax, jax.numpy as jnp
        import numpy as np
        UNITS = 128
        NUM_HEADS = 8

        def _split_heads(x, n):
            B, S, D = x.shape
            return x.reshape(B, S, n, D // n).transpose(0, 2, 1, 3)
        H = NUM_HEADS
        depth = UNITS // H
        Q = _split_heads(query, H) * depth ** (-0.5)
        k_mem, v_mem = jnp.split(memory, 2, axis=2)
        K = _split_heads(k_mem, H)
        V = _split_heads(v_mem, H)
        logits = jnp.einsum('bhqd,bhkd->bhqk', Q, K) + b[0]
        mask = seq_mask.astype(jnp.float32)[:, None, None, :]
        logits = logits + -1e+30 * (1.0 - mask)
        weights = jax.nn.softmax(logits, axis=-1)
        out = jnp.einsum('bhqk,bhkd->bhqd', weights, V)
        B, _, S, _ = out.shape
        return out.transpose(0, 2, 1, 3).reshape(B, S, UNITS)

    def _L1_ffn_ref(x, ln1_w, ln1_b, w_qkv, w_proj, ln2_w, ln2_b, gate_w, gate_b, w1, w2):
        import jax, jax.numpy as jnp
        import numpy as np
        B, N, D, H, E = (4, 128, 128, 16, 8)
        DK = D // H
        HID = 4 * D
        EPS = 1e-05

        def _layernorm(x, w, b):
            m = jnp.mean(x, axis=-1, keepdims=True)
            v = jnp.mean(jnp.square(x - m), axis=-1, keepdims=True)
            return (x - m) * jax.lax.rsqrt(v + EPS) * w + b

        def _msa(x, w_qkv, w_proj):
            b, n, d = x.shape
            qkv = (x @ w_qkv).reshape(b, n, 3, H, DK)
            q = qkv[:, :, 0].transpose(0, 2, 1, 3)
            k = qkv[:, :, 1].transpose(0, 2, 1, 3)
            v = qkv[:, :, 2].transpose(0, 2, 1, 3)
            attn = jnp.einsum('bhnd,bhmd->bhnm', q, k) * (1.0 / np.sqrt(DK))
            attn = jax.nn.softmax(attn, axis=-1)
            y = jnp.einsum('bhnm,bhmd->bhnd', attn, v)
            y = y.transpose(0, 2, 1, 3).reshape(b, n, d)
            return y @ w_proj

        def _moe_mlp(x, gate_w, gate_b, w1, w2):
            b, n, d = x.shape
            xf = x.reshape(b * n, d)
            logits = xf @ gate_w + gate_b
            one_hot = jax.nn.one_hot(jnp.argmax(logits, axis=-1), E, dtype=xf.dtype)
            h = jax.nn.gelu(jnp.einsum('td,edh->teh', xf, w1), approximate=True)
            y = jnp.einsum('teh,ehd->ted', h, w2)
            out = jnp.einsum('te,ted->td', one_hot, y)
            return out.reshape(b, n, d)
        x = x + _msa(_layernorm(x, ln1_w, ln1_b), w_qkv, w_proj)
        x = x + _moe_mlp(_layernorm(x, ln2_w, ln2_b), gate_w, gate_b, w1, w2)
        return x
    x = _layernorm(x + _L0_attn_ref(x, L0_attn_WQ_w, L0_attn_WQ_b, L0_attn_WK_w, L0_attn_WK_b, L0_attn_WV_w, L0_attn_WV_b, L0_attn_Wo_w, L0_attn_Wo_b), axis=-1)
    x = _layernorm(x + _L0_xattn_ref(x, ctx_2048, L0_xattn_w_qkv, L0_xattn_w_proj, L0_xattn_b_proj), axis=-1)
    x = _layernorm(x + _L0_ffn_ref(x, L0_ffn_moe_router, L0_ffn_moe_w13, L0_ffn_moe_w2), axis=-1)
    x = _layernorm(x + _L1_attn_ref(x, L1_attn_in_proj_w, L1_attn_conv_w, L1_attn_conv_b, L1_attn_x_proj_w, L1_attn_dt_head_w, L1_attn_dt_head_b, L1_attn_out_proj_w, L1_attn_D), axis=-1)
    x = _layernorm(x + _L1_xattn_ref(ctx_2048, x, mask_BxS2_ik0, L1_xattn_b), axis=-1)
    x = _layernorm(x + _L1_ffn_ref(x, L1_ffn_ln1_w, L1_ffn_ln1_b, L1_ffn_w_qkv, L1_ffn_w_proj, L1_ffn_ln2_w, L1_ffn_ln2_b, L1_ffn_gate_w, L1_ffn_gate_b, L1_ffn_w1, L1_ffn_w2), axis=-1)
    return x

_drawn_inputs = setup_inputs


def setup_inputs(seed=0):
    import zlib

    import numpy as np

    out = dict(_drawn_inputs(seed))
    spreads = {'L1_attn_conv_b': (0.0, 0.8),
     'L1_attn_D': (1.0, 0.6),
     'L1_ffn_ln1_w': (1.0, 0.6),
     'L1_ffn_ln1_b': (0.0, 0.8),
     'L1_ffn_ln2_w': (1.0, 0.6),
     'L1_ffn_ln2_b': (0.0, 0.653),
     'L1_ffn_gate_b': (0.0, 0.437)}
    factors = {'L0_attn_WQ_w': 8.0,
     'L0_attn_WQ_b': 8.0,
     'L0_attn_WK_w': 8.0,
     'L0_attn_WK_b': 8.0,
     'L0_attn_WV_w': 4.609,
     'L0_attn_WV_b': 8.0,
     'L0_attn_Wo_w': 4.398,
     'L0_attn_Wo_b': 3.059,
     'L0_xattn_w_qkv': 8.0,
     'L0_xattn_b_proj': 3.13,
     'L0_ffn_moe_router': 8.0,
     'L0_ffn_moe_w13': 8.0,
     'L0_ffn_moe_w2': 8.0,
     'L1_attn_in_proj_w': 8.0,
     'L1_attn_conv_w': 8.0,
     'L1_attn_x_proj_w': 8.0,
     'L1_attn_dt_head_w': 8.0,
     'L1_attn_dt_head_b': 32.994,
     'L1_attn_out_proj_w': 8.0,
     'L1_ffn_w_qkv': 3.84,
     'L1_ffn_w_proj': 3.773}
    for name, (base, spread) in spreads.items():
        noise = np.random.default_rng([zlib.crc32(name.encode()), seed]).standard_normal(out[name].shape)
        drawn = base * np.exp(spread * noise) if base else spread * noise
        out[name] = jnp.asarray(drawn.astype(out[name].dtype))
    for name, factor in factors.items():
        out[name] = (out[name] * factor).astype(out[name].dtype)
    return out
```

```python
from contextlib import ExitStack

import concourse.bass as bass
from concourse import mybir

ALU = mybir.AluOpType
ACT = mybir.ActivationFunctionType
AX = mybir.AxisListType
F32 = mybir.dt.float32
BF16 = mybir.dt.bfloat16
I32 = mybir.dt.int32

P = 128
EPS = 1e-5
NEG = -1e30
STREAMS = (0, 1)
DVE_STEPS = 134
LAYER_NORMS = 8
CTX_LOADS = 7 * 16

CONST_COLS = {"ident": 128, "causal": 64, "cos": 4, "sin": 4, "nsin": 4, "mask8": 8, "mask4": 4,
              "rank": 8, "select": 32, "ones": 128}
CONST_AT = {}
_at = 0
for _name, _n in CONST_COLS.items():
    CONST_AT[_name] = _at
    _at += _n
N_CONST = _at

PER_TILE = {
    "xT_psum": 7, "xT_ready": 7,
    "qkv_psum": 3, "rope_done": 1, "qkT_psum": 1, "qT_ready": 3, "kmask_ready": 3, "v_ready": 3,
    "ctxT_psum": 1, "ctxT_ready": 1, "ctx_used": 1, "ctx_values_ready": 1, "ctx_prepared": 1,
    "scores_psum": 5, "scores_shifted": 5, "probs_ready": 5, "probsT_psum": 5, "probsT_ready": 5,
    "heads_psum": 4, "heads_ready": 4, "headsT_psum": 3, "headsT_ready": 3, "projected": 3,
    "residual_biased": 3,
    "variance_ready": 8, "rstd_ready": 8, "normed": 8,
    "router_psum": 2, "top_diff": 1, "top_exp": 1, "logits_read": 2,
    "up_psum": 16, "act_ready": 16, "hidden_ready": 8, "down_psum": 16, "expert_added": 16,
    "in_psum": 1, "xpad_ready": 1, "conv_done": 1, "conv_silu": 1, "xdbl_psum": 1, "dt_low_ready": 1,
    "k_squared": 1, "dt_psum": 1, "tanh_ready": 1, "ksum_psum": 1, "kq_ready": 1, "kq_mid": 1, "kq_mid_copied": 1, "kq_split": 1,
    "kq_bc_psum": 4, "kq_bc_ready": 4, "xgain_ready": 1, "drive_ready": 2,
    "decay_raw": 2, "decay_ready": 2, "state_used": 2, "y_summed": 2, "y_ready": 1, "ssm_projected": 1,
}
ONCE = ["x_loaded0", "x_loaded1", "ctx_loaded0", "ctx_loaded1", "out_stored", "result_free", "weights_loaded", "expert_loaded", "late_loaded", "wT_psum", "wT_copied", "prepared_act", "prepared_dve",
        "prepared_pool", "dve_step", "cleared"]


def post_norm_decoder(nc, a, consts, out):
    B, S, D = a["x"].shape
    PAIRS = B * S // P // 2
    E = 8
    NH = 16
    DSTATE, DTR, DIN = 16, 64, 256

    with ExitStack() as ctx:
        def sb(name, shape, dt=F32):
            return ctx.enter_context(nc.sbuf_tensor(name, shape, dt))

        def two(name, shape, dt=F32):
            return [sb(f"{name}{s}", shape, dt) for s in STREAMS]

        sem = {n: ctx.enter_context(nc.semaphore(n)) for n in [*PER_TILE, *ONCE]}

        wide = [ctx.enter_context(nc.psum_tensor(f"wide{s}", [P, 2, 512], F32)) for s in STREAMS]
        misc = [ctx.enter_context(nc.psum_tensor(f"misc{s}", [P, 2, 512], F32)) for s in STREAMS]

        cst = sb("cst", [P, N_CONST])
        ident_b = sb("ident_b", [P, P], BF16)
        causal_b = sb("causal_b", [P, 64], BF16)
        select_b = sb("select_b", [96, 32], BF16)
        wqkvoT = sb("wqkvoT", [P, 4, P])
        wx = sb("wx", [P, 4, P])
        win = sb("win", [P, 4, P])
        wxp = sb("wxp", [P, 2, 96])
        wdt = sb("wdt", [DTR, 2, P])
        wout = sb("wout", [P, 2, P])
        wlast = sb("wlast", [P, 3 * P])
        wlproj = sb("wlproj", [P, P])
        router = sb("router", [P, E])
        gate_w = sb("gate_w", [P, E])
        w13 = sb("w13", [P, E, 512])
        w2 = sb("w2", [P, E, 2, P])
        w1 = sb("w1", [P, E, 512])
        w2b = sb("w2b", [P, E, 4, P])
        b_qk = sb("b_qk", [P, 2 * P])
        b_v = sb("b_v", [P, P])
        b_o = sb("b_o", [P, 2, P])
        ln_w = sb("ln_w", [P, 2, P])
        ln_b = sb("ln_b", [P, 2, P])
        gate_b = sb("gate_b", [P, E])
        mask_b = sb("mask_b", [P, 1])
        conv_w = sb("conv_w", [P, 2, 4])
        conv_b = sb("conv_b", [P, 2])
        dt_b = sb("dt_b", [P, 2])
        dt_bh = sb("dt_bh", [P, 2])
        skip_d = sb("skip_d", [P, 2])
        minus_half = sb("minus_half", [P, 1])

        X = two("X", [P, LAYER_NORMS + 1, P])
        XT = two("XT", [P, P])
        QK = two("QK", [P, 2 * P])
        QT = two("QT", [P, P])
        KC = two("KC", [P, 4, P])
        CTX = two("CTX", [P, 2 * P])
        CTXT = two("CTXT", [P, P])
        CV = two("CV", [P, 2, P])
        V1 = two("V1", [P, 2, NH, 9])
        V2 = two("V2", [P, 2, NH, 9])
        V5 = two("V5", [P, 2, 8, 17])
        PADI = two("PADI", [P, 64], I32)
        PAD = two("PAD", [P, 64])
        MX = two("MX", [P, NH])
        RC = two("RC", [P, NH])
        OH = two("OH", [P, P])
        OT = two("OT", [P, P])
        XB = two("XB", [P, P])
        R = two("R", [P, P])
        ST = two("ST", [P, 6])
        MV = two("MV", [P, 2])
        VE = two("VE", [P, 1])
        RS = two("RS", [P, 1])
        LG = two("LG", [P, 8, E])
        SM = two("SM", [P, 12])
        G = two("G", [P, E])
        XP = two("XP", [P, 2, 2, 67])
        XC = two("XC", [P, 2, P])
        XS = two("XS", [P, 2, P])
        ZS = two("ZS", [P, 2, P])
        DTL = two("DTL", [DTR, P])
        KKS = two("KKS", [32, P])
        RES = two("RES", [32, P])
        KQ = two("KQ", [32, P])
        KMID = two("KMID", [32, P], BF16)
        SPL = two("SPL", [96, P], BF16)
        TG = XC
        U = two("U", [P, 2, P])
        XU = two("XU", [P, 2, P])
        Y = two("Y", [P, 2, P])
        KB = two("KB", [P, DSTATE, P])
        KKB = two("KKB", [P, DSTATE, P])
        QB = two("QB", [P, DSTATE, P])
        DEC = two("DEC", [P, 2 * DSTATE, 64])
        DRV = two("DRV", [P, DSTATE, P])

        def part(buffers, first, last):
            return [t[:, first:last, :].rearrange("p a b -> p (a b)") for t in buffers]

        PR = part(KKB, 0, 8)
        PT = [t[:, 8:16, :] for t in KKB]
        KM = [t[:, 0:8, :] for t in DRV]
        KX = [t.rearrange("p (h b a k) -> p h b a k", h=8, b=2, a=2) for t in part(QB, 0, 16)]
        HT = [t.rearrange("p (e c t) -> p e c t", e=2, c=4) for t in part(KB, 0, 8)]
        ACTV = [t.rearrange("p (e f) -> p e f", e=2) for t in part(KB, 8, 12)]
        RA = part(KB, 12, 14)
        RB = part(KB, 14, 16)
        raw = [t[:, j, :] for t in (KB[0], KB[1]) for j in range(16)]

        def const(name, parts=P):
            return cst[0:parts, CONST_AT[name]:CONST_AT[name] + CONST_COLS[name]]

        ident = const("ident")
        one_col = const("ones")[:, 0:1]
        mask8 = const("mask8").unsqueeze(2)
        mask4 = const("mask4").unsqueeze(2)

        def value(pair):
            def at(name, k, s):
                n = PER_TILE[name]
                return pair * (2 * n) + (2 * k + s + 1)
            return at

        def wait_apart(engine, *waits):
            waits = [(sem[name], engine.to_reg(value)) for name, value in waits]
            engine.wait_ge(sem["prepared_dve"], 1)
            for semaphore, value in waits:
                engine.wait_ge(semaphore, value)

        x_tiles = a["x"].rearrange("(n c) s d -> n (c s) d", c=2)
        ctx_rows = a["ctx_2048"]
        ctx_tiles = ctx_rows.rearrange("(n c) s d -> n (c s) d", c=2)
        out_tiles = out.rearrange("(n c) s d -> n (c s) d", c=2)


        block = ctx.enter_context(nc.Block())

        @block.sync
        def _(sp):
            early_count = []

            def early(dst, src, slow=False):
                early_count.append(dst)
                sp.dma_start(dst, src, allow_slow_non_contiguous=slow).then_inc(sem["weights_loaded"], 16)

            def columns(name):
                return a[name].rearrange("(c p) -> p c", p=P)

            def load_tiles(pair):
                for s in STREAMS:
                    n = pair * 2 + s
                    sp.dma_start(X[s][:, 0, :], x_tiles[n]).then_inc(sem[f"x_loaded{s}"], 16)
                    sp.dma_start(CTX[s][:, :], ctx_tiles[n]).then_inc(sem[f"ctx_loaded{s}"], 16)
                    for b in range(2):
                        for half in range(2):
                            sp.dma_start(CV[s][half * 64:half * 64 + 64, b, :],
                                         ctx_rows[n * 2 + b][:, P:2 * P]).then_inc(sem[f"ctx_loaded{s}"], 16)
                        sp.dma_start(PADI[s][b * 64:b * 64 + 64, :],
                                     a["mask_BxS2_ik0"][n * 2 + b].partition_broadcast(64)
                                     ).then_inc(sem[f"ctx_loaded{s}"], 16)

            early(cst[:, :], consts)
            load_tiles(0)
            for j, n in enumerate(["WQ_w", "WK_w", "WV_w", "Wo_w"]):
                early(raw[j], a["L0_attn_" + n])
            early(KB[0][:, 4:7, :], a["L0_xattn_w_qkv"].rearrange("(c p) d -> p c d", p=P))
            early(KB[0][:, 7, :], a["L0_xattn_w_proj"])
            early(KB[0][:, 8:12, :], a["L1_attn_in_proj_w"].rearrange("(c p) d -> p c d", p=P))
            early(KB[0][0:96, 12:14, :], a["L1_attn_x_proj_w"].rearrange("r (c d) -> r c d", c=2))
            early(KB[0][:, 14:16, 0:DTR], a["L1_attn_dt_head_w"].rearrange("(c p) d -> p c d", p=P))
            early(KB[1][:, 0:2, :], a["L1_attn_out_proj_w"].rearrange("r (c d) -> r c d", c=2))
            early(b_qk[:, 0:P], a["L0_attn_WQ_b"].partition_broadcast(P))
            early(b_qk[:, P:2 * P], a["L0_attn_WK_b"].partition_broadcast(P))
            early(b_v[:, :], a["L0_attn_WV_b"].partition_broadcast(P))
            early(b_o[:, 0, :], a["L0_attn_Wo_b"].partition_broadcast(P))
            early(b_o[:, 1, :], a["L0_xattn_b_proj"].partition_broadcast(P))
            early(ln_w[:, 0, :], a["L1_ffn_ln1_w"].partition_broadcast(P))
            early(ln_w[:, 1, :], a["L1_ffn_ln2_w"].partition_broadcast(P))
            early(ln_b[:, 0, :], a["L1_ffn_ln1_b"].partition_broadcast(P))
            early(ln_b[:, 1, :], a["L1_ffn_ln2_b"].partition_broadcast(P))
            early(gate_b[:, :], a["L1_ffn_gate_b"].partition_broadcast(P))
            early(mask_b[:, :], a["L1_xattn_b"].partition_broadcast(P))
            early(conv_w[:, :, :], a["L1_attn_conv_w"].rearrange("(c p) o k -> p c (o k)", p=P))
            early(conv_b[:, :], columns("L1_attn_conv_b"), slow=True)
            early(dt_b[:, :], columns("L1_attn_dt_head_b"), slow=True)
            early(skip_d[:, :], columns("L1_attn_D"), slow=True)
            early(router[:, :], a["L0_ffn_moe_router"])
            early(gate_w[:, :], a["L1_ffn_gate_w"])
            early(wlast[:, :], a["L1_ffn_w_qkv"])
            early(wlproj[:, :], a["L1_ffn_w_proj"])
            assert len(early_count) == N_EARLY, len(early_count)
            for e in range(E):
                sp.dma_start(w13[:, e, :], a["L0_ffn_moe_w13"][e]).then_inc(sem["expert_loaded"], 16)
                sp.dma_start(w2[:, e, :, :], a["L0_ffn_moe_w2"][e].rearrange("(c p) d -> p c d", p=P)
                             ).then_inc(sem["expert_loaded"], 16)
            for e in range(E):
                sp.dma_start(w1[:, e, :], a["L1_ffn_w1"][e]).then_inc(sem["late_loaded"], 16)
                sp.dma_start(w2b[:, e, :, :], a["L1_ffn_w2"][e].rearrange("(c p) d -> p c d", p=P)
                             ).then_inc(sem["late_loaded"], 16)

            def store_tiles(pair):
                at = value(pair)
                for s in STREAMS:
                    sp.wait_ge(sem["normed"], at("normed", 7, s))
                    sp.dma_start(out_tiles[pair * 2 + s], X[s][:, LAYER_NORMS, :]).then_inc(sem["out_stored"], 16)

            with sp.Fori(0, PAIRS - 1) as pair:
                at = value(pair)
                sp.wait_ge(sem["normed"], at("normed", 0, 1))
                sp.wait_ge(sem["ctx_used"], at("ctx_used", 0, 1))
                sp.wait_ge(sem["ctx_values_ready"], at("ctx_values_ready", 0, 1))
                load_tiles(pair + 1)
                store_tiles(pair)
                sp.wait_ge(sem["out_stored"], (pair + 1) * 32)
                sp.sem_inc(sem["result_free"], 1)
            store_tiles(PAIRS - 1)
            sp.wait_ge(sem["out_stored"], 16 * 2 * PAIRS)

        @block.gpsimd
        def _(pool):
            nc.gpsimd.memset(minus_half[:, :], -0.5).then_inc(sem["prepared_pool"], 1)
            pool.wait_ge(sem["prepared_pool"], 1)
            pool.wait_ge(sem["weights_loaded"], N_EARLY * 16)
            pool.wait_ge(sem["prepared_dve"], 1)

            with pool.Fori(0, PAIRS) as pair:
                at = value(pair)

                def rstd(n):
                    for s in STREAMS:
                        pool.wait_ge(sem["variance_ready"], at("variance_ready", n, s))
                        nc.gpsimd.tensor_tensor(RS[s][:, :], VE[s][:, :], minus_half[:, :], ALU.pow
                                                ).then_inc(sem["rstd_ready"], 1)

                for s in STREAMS:
                    pool.wait_ge(sem[f"x_loaded{s}"], (pair + 1) * 16)
                    nc.gpsimd.tensor_tensor(XB[s][:, :], X[s][:, 0, :], b_o[:, 0, :], ALU.add
                                            ).then_inc(sem["residual_biased"], 1)
                for s in STREAMS:
                    pool.wait_ge(sem[f"ctx_loaded{s}"], (pair + 1) * CTX_LOADS)
                    pool.wait_ge(sem["ctxT_ready"], at("ctxT_ready", 0, s))
                    keys = CTXT[s][:, :].rearrange("p (b k) -> p b k", b=2).unsqueeze(1)
                    nc.gpsimd.tensor_tensor(KX[s][:, :, :, 0, :], keys.broadcast_to([P, 8, 2, 64]),
                                            mask8.unsqueeze(3).broadcast_to([P, 8, 2, 64]), ALU.mult)
                    nc.gpsimd.tensor_tensor(KC[s][:, :, :], CTXT[s][:, :].unsqueeze(1).broadcast_to([P, 4, P]),
                                            mask4.broadcast_to([P, 4, P]), ALU.mult)
                    nc.gpsimd.tensor_copy(V2[s][0:64, :, :, 0:8],
                                          CV[s][0:64, :, :].rearrange("p b (h d) -> p b h d", d=8))
                    nc.gpsimd.tensor_scalar(PAD[s][:, :], PADI[s][:, :], -4 * NEG, 4 * NEG, ALU.mult, ALU.add
                                            ).then_inc(sem["ctx_used"], 1)
                for s in STREAMS:
                    wait_apart(pool, ("ctx_used", at("ctx_used", 0, s)))
                    nc.gpsimd.tensor_scalar(PAD[s][:, :], PAD[s][:, :], mask_b[:, 0:1], None, ALU.add
                                            ).then_inc(sem["ctx_prepared"], 1)
                rstd(0)
                for s in STREAMS:
                    pool.wait_ge(sem["normed"], at("normed", 0, s))
                    nc.gpsimd.tensor_tensor(XB[s][:, :], X[s][:, 1, :], b_o[:, 1, :], ALU.add
                                            ).then_inc(sem["residual_biased"], 1)
                rstd(1)
                rstd(2)
                for c in range(2):
                    for s in STREAMS:
                        if c == 0:
                            pool.wait_ge(sem["kq_bc_ready"], at("kq_bc_ready", 3, s))
                            pool.wait_ge(sem["xgain_ready"], at("xgain_ready", 0, s))
                        else:
                            pool.wait_ge(sem["y_summed"], at("y_summed", 0, s))
                        nc.gpsimd.tensor_tensor(DRV[s][:, :, :], KB[s][:, :, :],
                                                XU[s][:, c, :].unsqueeze(1).broadcast_to([P, DSTATE, P]),
                                                ALU.mult).then_inc(sem["drive_ready"], 1)
                for n in range(3, 7):
                    rstd(n)
                for s in STREAMS:
                    pool.wait_ge(sem["normed"], at("normed", 6, s))
                    nc.gpsimd.tensor_tensor(XB[s][:, :], R[s][:, :], X[s][:, 5, :], ALU.add
                                            ).then_inc(sem["residual_biased"], 1)
                rstd(7)

        @block.scalar
        def _(act):
            act.wait_ge(sem["weights_loaded"], N_EARLY * 16)
            nc.scalar.copy(ident_b[:, :], ident)
            nc.scalar.copy(causal_b[:, :], const("causal"))
            nc.scalar.mul(dt_bh[:, :], dt_b[:, :], 0.5)
            nc.scalar.copy(select_b[:, :], const("select", 96)).then_inc(sem["prepared_act"], 1)

            with act.Fori(0, PAIRS) as pair:
                at = value(pair)

                def x_transposed(i):
                    for s in STREAMS:
                        act.wait_ge(sem["xT_psum"], at("xT_psum", i, s))
                        nc.scalar.copy(XT[s][:, :], misc[s][:, 0, 0:P]).then_inc(sem["xT_ready"], 1)

                def softmax(k, n, scale):
                    for s in STREAMS:
                        act.wait_ge(sem["scores_shifted"], at("scores_shifted", k, s))
                        nc.scalar.activation(PR[s][:, 0:n], PR[s][:, 0:n], ACT.Exp, scale=scale
                                             ).then_inc(sem["probs_ready"], 1)
                    for s in STREAMS:
                        act.wait_ge(sem["probsT_psum"], at("probsT_psum", k, s))
                        nc.scalar.copy(PT[s][:, 0:n // P, :].rearrange("p a b -> p (a b)"),
                                       wide[s][:, :, :].rearrange("p a b -> p (a b)")[:, 0:n]
                                       ).then_inc(sem["probsT_ready"], 1)

                def heads_transposed(i):
                    for s in STREAMS:
                        act.wait_ge(sem["headsT_psum"], at("headsT_psum", i, s))
                        nc.scalar.copy(OT[s][:, :], misc[s][:, 0, 0:P]).then_inc(sem["headsT_ready"], 1)

                act.wait_ge(sem["prepared_dve"], 1)
                for s in STREAMS:
                    act.wait_ge(sem[f"ctx_loaded{s}"], (pair + 1) * CTX_LOADS)
                    act.wait_ge(sem["ctxT_psum"], at("ctxT_psum", 0, s))
                    nc.scalar.copy(CTXT[s][:, :], misc[s][:, 0, 0:P]).then_inc(sem["ctxT_ready"], 1)
                    for half in range(2):
                        rows = slice(half * 64, half * 64 + 64)
                        i = nc.scalar.copy(
                            V5[s][rows, :, half:8:2, 0:16],
                            CV[s][rows, :, :].rearrange("p b (h d) -> p b h d", d=16)[:, :, half:8:2, :])
                    i.then_inc(sem["ctx_values_ready"], 1)
                x_transposed(0)
                for s in STREAMS:
                    act.wait_ge(sem["qkT_psum"], at("qkT_psum", 0, s))
                    nc.scalar.copy(QT[s][:, :], misc[s][:, 0, 0:P]).then_inc(sem["qT_ready"], 1)
                softmax(0, 1024, 8 ** -0.5)
                heads_transposed(0)
                x_transposed(1)
                for s in STREAMS:
                    act.wait_ge(sem["qkv_psum"], at("qkv_psum", 1, s))
                    nc.scalar.copy(QT[s][:, :], misc[s][:, 1, 0:P]).then_inc(sem["qT_ready"], 1)
                    nc.scalar.copy(V2[s][64:P, :, :, 0:8],
                                   misc[s][64:P, 1, 256:512].rearrange("p (b h d) -> p b h d", b=2, d=8)
                                   ).then_inc(sem["v_ready"], 1)
                softmax(1, 1024, 8 ** -0.5)
                softmax(2, 1024, 8 ** -0.5)
                heads_transposed(1)
                x_transposed(2)
                for s in STREAMS:
                    act.wait_ge(sem["top_diff"], at("top_diff", 0, s))
                    nc.scalar.activation(SM[s][:, 5:6], SM[s][:, 4:5], ACT.Exp).then_inc(sem["top_exp"], 1)
                for e in range(E):
                    for s in STREAMS:
                        act.wait_ge(sem["up_psum"], at("up_psum", e, s))
                        nc.scalar.activation(ACTV[s][:, e % 2, :], wide[s][:, e % 2, 0:256], ACT.Silu
                                             ).then_inc(sem["act_ready"], 1)
                x_transposed(3)
                for s in STREAMS:
                    act.wait_ge(sem["in_psum"], at("in_psum", 0, s))
                    nc.scalar.copy(XP[s][:, :, :, 3:67].rearrange("p c b t -> p (c b) t"),
                                   misc[s][:, 1, 0:256].rearrange("p (c t) -> p c t", t=64)
                                   ).then_inc(sem["xpad_ready"], 1)
                for s in STREAMS:
                    nc.scalar.activation(ZS[s][:, :, :].rearrange("p c t -> p (c t)"), misc[s][:, 1, 256:512], ACT.Silu)
                for s in STREAMS:
                    act.wait_ge(sem["conv_done"], at("conv_done", 0, s))
                    nc.scalar.activation(XS[s][:, :, :], XC[s][:, :, :], ACT.Silu).then_inc(sem["conv_silu"], 1)
                for s in STREAMS:
                    act.wait_ge(sem["xdbl_psum"], at("xdbl_psum", 0, s))
                    nc.scalar.copy(DTL[s][:, :], misc[s][0:DTR, 0, 128:256]).then_inc(sem["dt_low_ready"], 1)
                    nc.scalar.copy(KQ[s][:, :], misc[s][0:32, 0, 256:384]).then_inc(sem["kq_ready"], 1)
                    nc.scalar.activation(KKS[s][:, :], misc[s][0:32, 0, 256:384], ACT.Square
                                         ).then_inc(sem["k_squared"], 1)
                for s in STREAMS:
                    act.wait_ge(sem["kq_mid"], at("kq_mid", 0, s))
                    nc.scalar.copy(SPL[s][32:64, :], KMID[s][:, :]).then_inc(sem["kq_mid_copied"], 1)
                for s in STREAMS:
                    act.wait_ge(sem["dt_psum"], at("dt_psum", 0, s))
                    for c in range(2):
                        last = nc.scalar.activation(TG[s][:, c, :], misc[s][:, 1, c * P:c * P + P], ACT.Tanh,
                                                    bias=dt_bh[:, c:c + 1], scale=0.5)
                    last.then_inc(sem["tanh_ready"], 1)
                for g in range(4):
                    for s in STREAMS:
                        act.wait_ge(sem["kq_bc_psum"], at("kq_bc_psum", g, s))
                        flat = lambda t: t[s][:, 4 * g:4 * g + 4, :].rearrange("p n t -> p (n t)")
                        nc.scalar.copy(flat(KB), wide[s][:, 0, :])
                        nc.scalar.activation(flat(KKB), wide[s][:, 0, :], ACT.Square)
                        nc.scalar.copy(flat(QB), wide[s][:, 1, :]).then_inc(sem["kq_bc_ready"], 1)
                for c in range(2):
                    for s in STREAMS:
                        act.wait_ge(sem["decay_raw"], at("decay_raw", c, s))
                        nc.scalar.activation(DEC[s][:, :, 1:64], DEC[s][:, :, 1:64], ACT.Identity,
                                             bias=one_col, scale=-1.0).then_inc(sem["decay_ready"], 1)
                x_transposed(4)
                softmax(3, 512, 0.25)
                x_transposed(5)
                for s in STREAMS:
                    act.wait_ge(sem["qkv_psum"], at("qkv_psum", 2, s))
                    nc.scalar.copy(QT[s][:, :], misc[s][:, 1, 0:P]).then_inc(sem["qT_ready"], 1)
                    for half in range(2):
                        rows = slice(half * 64, half * 64 + 64)
                        i = nc.scalar.copy(
                            V1[s][rows, :, half:NH:2, 0:8],
                            misc[s][rows, 1, 256:512].rearrange("p (b h d) -> p b h d", b=2, d=8)[:, :, half:NH:2, :])
                    i.then_inc(sem["v_ready"], 1)
                softmax(4, 1024, 8 ** -0.5)
                heads_transposed(2)
                x_transposed(6)
                for e in range(E):
                    for s in STREAMS:
                        act.wait_ge(sem["up_psum"], at("up_psum", E + e, s))
                        nc.scalar.activation(HT[s][:, e % 2, :, :].rearrange("p c t -> p (c t)"), wide[s][:, e % 2, :],
                                             ACT.Gelu_apprx_tanh).then_inc(sem["act_ready"], 1)

        @block.vector
        def _(dve):
            for s in STREAMS:
                for t in (V1, V2, V5, XP, DEC):
                    nc.vector.memset(t[s][:], 0.0).then_inc(sem["cleared"], 1)
            dve.wait_ge(sem["cleared"], 10)
            nc.vector.memset(R[0][:, 0:1], 0.0).then_inc(sem["result_free"], 1)
            for s in STREAMS:
                nc.vector.memset(V1[s][0:64, :, 0:NH:2, 8:9], 1.0)
                nc.vector.memset(V1[s][64:P, :, 1:NH:2, 8:9], 1.0)
                nc.vector.memset(V2[s][:, :, :, 8:9], 1.0)
                nc.vector.memset(V5[s][0:64, :, 0:8:2, 16:17], 1.0)
                nc.vector.memset(V5[s][64:P, :, 1:8:2, 16:17], 1.0)
            dve.wait_ge(sem["weights_loaded"], N_EARLY * 16)
            nc.vector.tensor_scalar(mask_b[:, :], mask_b[:, :], 4.0, None, ALU.mult).then_inc(sem["prepared_dve"], 1)
            targets = [(wqkvoT, 0, 4, P, P), (wx, 0, 4, P, P), (win, 0, 4, P, P)]
            for g, (dst, _, n, _, _) in enumerate(targets):
                dve.wait_ge(sem["wT_psum"], g + 1)
                nc.vector.tensor_copy(dst[:, :, :], wide[g % 2][:, 0, :].rearrange("p (a b) -> p a b", a=4)
                                      ).then_inc(sem["wT_copied"], 1)
            dve.wait_ge(sem["wT_psum"], 4)
            nc.vector.tensor_copy(wxp[:, :, :], misc[0][:, 0, 0:256].rearrange("p (a b) -> p a b", a=2)[:, :, 0:96])
            nc.vector.tensor_copy(wdt[:, :, :], misc[0][0:DTR, 0, 256:512].rearrange("p (a b) -> p a b", a=2))
            nc.vector.tensor_copy(wout[:, :, :], misc[0][:, 1, 0:256].rearrange("p (a b) -> p a b", a=2)
                                  ).then_inc(sem["wT_copied"], 1)

            with dve.Fori(0, PAIRS) as pair:
                at = value(pair)
                count = [0]
                last = {}

                def step(instruction, s):
                    instruction.then_inc(sem["dve_step"], 1)
                    count[0] += 1
                    last[s] = count[0]

                def previous(s):
                    dve.wait_ge(sem["dve_step"], pair * DVE_STEPS + last[s])

                def norm(n, source, affine=None, experts=None):
                    for s in STREAMS:
                        if experts is None:
                            previous(s)
                        else:
                            dve.wait_ge(sem["expert_added"], at("expert_added", experts, s))
                        step(nc.vector.bn_stats(ST[s][:, :], source(s)), s)
                    for s in STREAMS:
                        wait_apart(dve, ("dve_step", pair * DVE_STEPS + last[s]))
                        step(nc.vector.bn_aggr(MV[s][:, :], ST[s][:, :]), s)
                    for s in STREAMS:
                        previous(s)
                        nc.vector.tensor_scalar(VE[s][:, :], MV[s][:, 1:2], EPS, None, ALU.add
                                                ).then_inc(sem["variance_ready"], 1)
                    for s in STREAMS:
                        dve.wait_ge(sem["rstd_ready"], at("rstd_ready", n, s))
                        i = nc.vector.tensor_scalar(X[s][:, n + 1, :], source(s), MV[s][:, 0:1], RS[s][:, 0:1],
                                                    ALU.subtract, ALU.mult)
                        if affine is None:
                            i.then_inc(sem["normed"], 1)
                        else:
                            step(i, s)
                    if affine is not None:
                        for s in STREAMS:
                            previous(s)
                            step(nc.vector.tensor_tensor(X[s][:, n + 1, :], X[s][:, n + 1, :], ln_w[:, affine, :],
                                                         ALU.mult), s)
                        for s in STREAMS:
                            previous(s)
                            nc.vector.tensor_tensor(X[s][:, n + 1, :], X[s][:, n + 1, :], ln_b[:, affine, :],
                                                    ALU.add).then_inc(sem["normed"], 1)

                def shift(k, heads, keys):
                    n = heads * keys // 2
                    for s in STREAMS:
                        dve.wait_ge(sem["scores_psum"], at("scores_psum", k, s))
                        sc = wide[s][:, :, 0:n].rearrange("p a (h k) -> p a h k", k=keys)
                        step(nc.vector.tensor_reduce(MX[s][:, 0:heads].rearrange("p (a h) -> p a h", a=2), sc,
                                                     AX.X, ALU.max), s)
                    for s in STREAMS:
                        previous(s)
                        for half in range(2):
                            h = heads // 2
                            i = nc.vector.tensor_tensor(
                                PR[s][:, half * n:half * n + n].rearrange("p (h k) -> p h k", k=keys),
                                wide[s][:, half, 0:n].rearrange("p (h k) -> p h k", k=keys),
                                MX[s][:, half * h:half * h + h].unsqueeze(2).broadcast_to([P, h, keys]), ALU.subtract)
                        i.then_inc(sem["scores_shifted"], 1)

                def heads_normed(i, heads, width):
                    for s in STREAMS:
                        dve.wait_ge(sem["heads_psum"], at("heads_psum", i, s))
                        o = misc[s][:, 1, 0:heads * (width + 1)].rearrange("p (h d) -> p h d", d=width + 1)
                        step(nc.vector.reciprocal(RC[s][:, 0:heads].unsqueeze(2), o[:, :, width:width + 1]), s)
                    for s in STREAMS:
                        previous(s)
                        o = misc[s][:, 1, 0:heads * (width + 1)].rearrange("p (h d) -> p h d", d=width + 1)
                        nc.vector.tensor_tensor(OH[s][:, :].rearrange("p (h d) -> p h d", d=width), o[:, :, 0:width],
                                                RC[s][:, 0:heads].unsqueeze(2).broadcast_to([P, heads, width]),
                                                ALU.mult).then_inc(sem["heads_ready"], 1)

                def mask_keys(i, source):
                    for s in STREAMS:
                        kt, ready, k = source
                        dve.wait_ge(sem[ready], at(ready, k, s))
                        nc.vector.tensor_tensor(KM[s], kt(s).unsqueeze(1).broadcast_to([P, 8, P]),
                                                mask8.broadcast_to([P, 8, P]), ALU.mult
                                                ).then_inc(sem["kmask_ready"], 1)

                for s in STREAMS:
                    dve.wait_ge(sem["qkv_psum"], at("qkv_psum", 0, s))
                    step(nc.vector.tensor_tensor(QK[s][:, :], misc[s][:, 1, 0:256], b_qk[:, :], ALU.add), s)
                for s in STREAMS:
                    previous(s)
                    pairs = lambda t: t[s][:, :].rearrange("p (h j d) -> p h j d", j=2, d=4)
                    wave = lambda n: const(n).unsqueeze(1).broadcast_to([P, 32, 4])
                    nc.vector.tensor_tensor(pairs(RA)[:, :, 0, :], pairs(QK)[:, :, 0, :], wave("cos"), ALU.mult)
                    nc.vector.tensor_tensor(pairs(RA)[:, :, 1, :], pairs(QK)[:, :, 1, :], wave("cos"), ALU.mult)
                    nc.vector.tensor_tensor(pairs(RB)[:, :, 0, :], pairs(QK)[:, :, 1, :], wave("nsin"), ALU.mult)
                    step(nc.vector.tensor_tensor(pairs(RB)[:, :, 1, :], pairs(QK)[:, :, 0, :], wave("sin"), ALU.mult), s)
                for s in STREAMS:
                    previous(s)
                    nc.vector.tensor_tensor(QK[s][:, :], RA[s][:, :], RB[s][:, :], ALU.add).then_inc(sem["rope_done"], 1)
                for s in STREAMS:
                    for half in range(2):
                        rows = slice(half * 64, half * 64 + 64)
                        split = lambda t: t.rearrange("p (h d) -> p h d", d=8)[:, half:NH:2, :]
                        for b in range(2):
                            i = nc.vector.tensor_tensor(V1[s][rows, b, half:NH:2, 0:8],
                                                        split(misc[s][rows, 1, 256 + b * P:256 + b * P + P]),
                                                        split(b_v[rows, :]), ALU.add)
                    i.then_inc(sem["v_ready"], 1)
                mask_keys(0, (lambda s: misc[s][:, 1, 0:P], "qkT_psum", 0))
                shift(0, NH, 64)
                heads_normed(0, NH, 8)
                for s in STREAMS:
                    dve.wait_ge(sem["projected"], at("projected", 0, s))
                    dve.wait_ge(sem["residual_biased"], at("residual_biased", 0, s))
                    step(nc.vector.tensor_tensor(R[s][:, :], misc[s][:, 0, P:2 * P], XB[s][:, :], ALU.add), s)
                norm(0, lambda s: R[s][:, :])

                for s in STREAMS:
                    dve.wait_ge(sem["qkv_psum"], at("qkv_psum", 1, s))
                    dve.wait_ge(sem["ctx_prepared"], at("ctx_prepared", 0, s))
                    keys = misc[s][:, 0, P:2 * P].rearrange("p (b k) -> p b k", b=2).unsqueeze(1)
                    nc.vector.tensor_tensor(KX[s][:, :, :, 1, :], keys.broadcast_to([P, 8, 2, 64]),
                                            mask8.unsqueeze(3).broadcast_to([P, 8, 2, 64]), ALU.mult
                                            ).then_inc(sem["kmask_ready"], 1)
                shift(1, 8, 128)
                shift(2, 8, 128)
                heads_normed(1, NH, 8)
                for s in STREAMS:
                    dve.wait_ge(sem["projected"], at("projected", 1, s))
                    dve.wait_ge(sem["residual_biased"], at("residual_biased", 1, s))
                    step(nc.vector.tensor_tensor(R[s][:, :], misc[s][:, 0, P:2 * P], XB[s][:, :], ALU.add), s)
                norm(1, lambda s: R[s][:, :])

                def best(logits, top, ranked, rank_max, hot, layer=None):
                    for s in STREAMS:
                        if layer is None:
                            previous(s)
                        else:
                            dve.wait_ge(sem["logits_read"], at("logits_read", layer, s))
                        step(nc.vector.tensor_reduce(SM[s][:, top:top + 1], LG[s][:, logits, :], AX.X, ALU.max), s)
                    for s in STREAMS:
                        previous(s)
                        step(nc.vector.scalar_tensor_tensor(
                            out=LG[s][:, ranked, :], in0=LG[s][:, logits, :], scalar=SM[s][:, top:top + 1],
                            in1=const("rank"), op0=ALU.is_ge, op1=ALU.mult), s)
                    for s in STREAMS:
                        previous(s)
                        step(nc.vector.tensor_reduce(SM[s][:, rank_max:rank_max + 1], LG[s][:, ranked, :], AX.X,
                                                     ALU.max), s)
                    for s in STREAMS:
                        previous(s)
                        step(nc.vector.tensor_scalar(hot(s), LG[s][:, ranked, :], SM[s][:, rank_max:rank_max + 1],
                                                     None, ALU.is_equal), s)

                for s in STREAMS:
                    dve.wait_ge(sem["router_psum"], at("router_psum", 0, s))
                    nc.vector.tensor_copy(LG[s][:, 0, :], misc[s][:, 1, 0:E]).then_inc(sem["logits_read"], 1)
                best(0, 0, 1, 1, lambda s: LG[s][:, 2, :], 0)
                for s in STREAMS:
                    previous(s)
                    step(nc.vector.scalar_tensor_tensor(out=LG[s][:, 3, :], in0=LG[s][:, 2, :], scalar=NEG,
                                                        in1=LG[s][:, 0, :], op0=ALU.mult, op1=ALU.add), s)
                best(3, 2, 4, 3, lambda s: LG[s][:, 5, :])
                for s in STREAMS:
                    nc.vector.tensor_tensor(SM[s][:, 4:5], SM[s][:, 2:3], SM[s][:, 0:1], ALU.subtract
                                            ).then_inc(sem["top_diff"], 1)
                for s in STREAMS:
                    dve.wait_ge(sem["top_exp"], at("top_exp", 0, s))
                    step(nc.vector.tensor_scalar(SM[s][:, 6:7], SM[s][:, 5:6], 1.0, None, ALU.add), s)
                for s in STREAMS:
                    previous(s)
                    step(nc.vector.reciprocal(SM[s][:, 7:8], SM[s][:, 6:7]), s)
                for s in STREAMS:
                    previous(s)
                    nc.vector.tensor_tensor(SM[s][:, 8:9], SM[s][:, 7:8], SM[s][:, 5:6], ALU.mult)
                    step(nc.vector.tensor_scalar(LG[s][:, 6, :], LG[s][:, 2, :], SM[s][:, 7:8], None, ALU.mult), s)
                for s in STREAMS:
                    previous(s)
                    step(nc.vector.scalar_tensor_tensor(out=G[s][:, :], in0=LG[s][:, 5, :], scalar=SM[s][:, 8:9],
                                                        in1=LG[s][:, 6, :], op0=ALU.mult, op1=ALU.add), s)

                def add_expert(k, e, before=None):
                    for s in STREAMS:
                        dve.wait_ge(sem["down_psum"], at("down_psum", k, s))
                        if e == 0:
                            previous(s)
                        else:
                            dve.wait_ge(sem["expert_added"], at("expert_added", k - 1, s))
                        nc.vector.scalar_tensor_tensor(
                            out=R[s][:, :], in0=misc[s][:, e % 2, 256:384], scalar=G[s][:, e:e + 1],
                            in1=(before(s) if before else R[s][:, :]), op0=ALU.mult, op1=ALU.add
                        ).then_inc(sem["expert_added"], 1)

                def gated(e):
                    for s in STREAMS:
                        dve.wait_ge(sem["act_ready"], at("act_ready", e, s))
                        nc.vector.tensor_tensor(HT[s][:, e % 2, 0:2, :].rearrange("p c t -> p (c t)"),
                                                ACTV[s][:, e % 2, :], wide[s][:, e % 2, 256:512], ALU.mult
                                                ).then_inc(sem["hidden_ready"], 1)

                gated(0)
                for e in range(1, E):
                    gated(e)
                    add_expert(e - 1, e - 1, (lambda s: X[s][:, 2, :]) if e == 1 else None)
                add_expert(E - 1, E - 1)
                norm(2, lambda s: R[s][:, :], experts=E - 1)

                for s in STREAMS:
                    dve.wait_ge(sem["xpad_ready"], at("xpad_ready", 0, s))
                    for c in range(2):
                        i = nc.vector.tensor_scalar(XC[s][:, c, :].rearrange("p (b t) -> p b t", b=2),
                                                    XP[s][:, c, :, 0:64], conv_w[:, c, 0:1], conv_b[:, c:c + 1],
                                                    ALU.mult, ALU.add)
                    step(i, s)
                for j in range(1, 4):
                    for s in STREAMS:
                        previous(s)
                        for c in range(2):
                            xc = XC[s][:, c, :].rearrange("p (b t) -> p b t", b=2)
                            i = nc.vector.scalar_tensor_tensor(out=xc, in0=XP[s][:, c, :, j:j + 64],
                                                               scalar=conv_w[:, c, j:j + 1], in1=xc,
                                                               op0=ALU.mult, op1=ALU.add)
                        if j < 3:
                            step(i, s)
                        else:
                            i.then_inc(sem["conv_done"], 1)
                for s in STREAMS:
                    dve.wait_ge(sem["kq_ready"], at("kq_ready", 0, s))
                    step(nc.vector.tensor_copy(SPL[s][0:32, :], KQ[s][:, :]), s)
                for s in STREAMS:
                    previous(s)
                    step(nc.vector.tensor_tensor(RES[s][:, :], KQ[s][:, :], SPL[s][0:32, :],
                                                 ALU.subtract), s)
                for s in STREAMS:
                    previous(s)
                    nc.vector.tensor_copy(KMID[s][:, :], RES[s][:, :]).then_inc(sem["kq_mid"], 1)
                for s in STREAMS:
                    dve.wait_ge(sem["kq_mid"], at("kq_mid", 0, s))
                    nc.vector.tensor_tensor(SPL[s][64:96, :], RES[s][:, :], KMID[s][:, :], ALU.subtract
                                            ).then_inc(sem["kq_split"], 1)
                both = lambda t: t.unsqueeze(1).broadcast_to([P, 2, P])
                for s in STREAMS:
                    dve.wait_ge(sem["tanh_ready"], at("tanh_ready", 0, s))
                    dve.wait_ge(sem["ksum_psum"], at("ksum_psum", 0, s))
                    step(nc.vector.tensor_scalar(TG[s][:, :, :], TG[s][:, :, :], 0.5, 0.5, ALU.mult, ALU.add), s)
                for s in STREAMS:
                    previous(s)
                    step(nc.vector.tensor_tensor(XU[s][:, :, :], TG[s][:, :, :], both(misc[s][:, 0, 384:512]),
                                                 ALU.mult), s)
                for s in STREAMS:
                    previous(s)
                    step(nc.vector.tensor_scalar(XU[s][:, :, :], XU[s][:, :, :], 1.0, None, ALU.add), s)
                for s in STREAMS:
                    previous(s)
                    step(nc.vector.reciprocal(XU[s][:, :, :], XU[s][:, :, :]), s)
                for s in STREAMS:
                    previous(s)
                    step(nc.vector.tensor_tensor(U[s][:, :, :], TG[s][:, :, :], XU[s][:, :, :], ALU.mult), s)
                for s in STREAMS:
                    previous(s)
                    nc.vector.tensor_tensor(XU[s][:, :, :], XS[s][:, :, :], U[s][:, :, :], ALU.mult
                                            ).then_inc(sem["xgain_ready"], 1)
                for c in range(2):
                    for s in STREAMS:
                        if c == 0:
                            dve.wait_ge(sem["kq_bc_ready"], at("kq_bc_ready", 3, s))
                        rows = lambda t: t.rearrange("p n (b t) -> p n b t", b=2)[:, :, :, 1:64]
                        nc.vector.tensor_tensor(
                            DEC[s][:, :, :].rearrange("p (n b) t -> p n b t", b=2)[:, :, :, 1:64], rows(KKB[s][:, :, :]),
                            rows(U[s][:, c:c + 1, :]).broadcast_to([P, DSTATE, 2, 63]), ALU.mult).then_inc(sem["decay_raw"], 1)
                    for s in STREAMS:
                        dve.wait_ge(sem["decay_ready"], at("decay_ready", c, s))
                        dve.wait_ge(sem["drive_ready"], at("drive_ready", c, s))
                        drv = DRV[s][:, :, :].rearrange("p n t -> p (n t)")
                        step(nc.vector.tensor_tensor_scan(drv, DEC[s][:, :, :].rearrange("p n t -> p (n t)"), drv, 0.0,
                                                          ALU.mult, ALU.add), s)
                    for s in STREAMS:
                        previous(s)
                        nc.vector.tensor_tensor(DRV[s][:, :, :], DRV[s][:, :, :], QB[s][:, :, :], ALU.mult
                                                ).then_inc(sem["state_used"], 1)
                    for s in STREAMS:
                        dve.wait_ge(sem["state_used"], at("state_used", c, s))
                        nc.vector.tensor_reduce(Y[s][:, c, :], DRV[s][:, :, :].rearrange("p n t -> p t n"), AX.X,
                                                ALU.add).then_inc(sem["y_summed"], 1)
                for c in range(2):
                    for s in STREAMS:
                        dve.wait_ge(sem["y_summed"], at("y_summed", 1, s))
                        step(nc.vector.scalar_tensor_tensor(out=Y[s][:, c, :], in0=XS[s][:, c, :],
                                                            scalar=skip_d[:, c:c + 1], in1=Y[s][:, c, :],
                                                            op0=ALU.mult, op1=ALU.add), s)
                for s in STREAMS:
                    previous(s)
                    nc.vector.tensor_tensor(Y[s][:, :, :], Y[s][:, :, :], ZS[s][:, :, :], ALU.mult
                                            ).then_inc(sem["y_ready"], 1)
                for s in STREAMS:
                    dve.wait_ge(sem["ssm_projected"], at("ssm_projected", 0, s))
                    step(nc.vector.tensor_tensor(R[s][:, :], misc[s][:, 0, 0:P], X[s][:, 3, :], ALU.add), s)
                norm(3, lambda s: R[s][:, :])

                shift(3, 8, 64)
                heads_normed(3 - 1, 8, 16)
                for s in STREAMS:
                    dve.wait_ge(sem["heads_ready"], at("heads_ready", 2, s))
                    step(nc.vector.tensor_tensor(R[s][:, :], OH[s][:, :], X[s][:, 4, :], ALU.add), s)
                norm(4, lambda s: R[s][:, :])

                dve.wait_ge(sem["normed"], at("normed", 4, 1))
                norm(5, lambda s: X[s][:, 5, :], affine=0)
                mask_keys(2, (lambda s: misc[s][:, 0, P:2 * P], "qkv_psum", 2))
                shift(4, NH, 64)
                heads_normed(3, NH, 8)
                for s in STREAMS:
                    dve.wait_ge(sem["projected"], at("projected", 2, s))
                    step(nc.vector.tensor_tensor(R[s][:, :], misc[s][:, 0, P:2 * P], X[s][:, 5, :], ALU.add), s)
                norm(6, lambda s: R[s][:, :], affine=1)
                for s in STREAMS:
                    dve.wait_ge(sem["router_psum"], at("router_psum", 1, s))
                    nc.vector.tensor_tensor(LG[s][:, 0, :], misc[s][:, 1, 0:E], gate_b[:, :], ALU.add
                                            ).then_inc(sem["logits_read"], 1)
                best(0, 0, 1, 1, lambda s: G[s][:, :], 1)
                dve.wait_ge(sem["residual_biased"], at("residual_biased", 2, 1))
                for e in range(E):
                    add_expert(E + e, e, (lambda s: XB[s][:, :]) if e == 0 else None)
                dve.wait_ge(sem["result_free"], pair + 1)
                norm(7, lambda s: R[s][:, :], experts=2 * E - 1)
                assert count[0] == DVE_STEPS, count[0]

        @block.tensor
        def _(pe):
            pe.wait_ge(sem["weights_loaded"], N_EARLY * 16)
            for g in range(3):
                if g == 2:
                    pe.wait_ge(sem["wT_copied"], 1)
                for j in range(4):
                    i = nc.tensor.transpose(wide[g % 2][:, 0, j * P:j * P + P], raw[4 * g + j], ident)
                i.then_inc(sem["wT_psum"], 1)
            for j in range(2):
                nc.tensor.transpose(misc[0][:, 0, j * P:j * P + 96], raw[12 + j][0:96, :], ident[0:96, 0:96])
                nc.tensor.transpose(misc[0][0:DTR, 0, 256 + j * P:256 + j * P + P], raw[14 + j][:, 0:DTR], ident)
                i = nc.tensor.transpose(misc[0][:, 1, j * P:j * P + P], raw[16 + j], ident)
            i.then_inc(sem["wT_psum"], 1)
            pe.wait_ge(sem["wT_copied"], 4)
            pe.wait_ge(sem["prepared_act"], 1)
            pe.wait_ge(sem["prepared_dve"], 1)

            with pe.Fori(0, PAIRS) as pair:
                at = value(pair)

                def mm(out_, lhsT, rhs, start=True, stop=True):
                    return nc.tensor.matmul(out_, lhsT, rhs, start=start, stop=stop, skip_group_check=True)

                def transpose_x(i, n):
                    for s in STREAMS:
                        if n:
                            pe.wait_ge(sem["normed"], at("normed", n - 1, s))
                        nc.tensor.transpose(misc[s][:, 0, 0:P], X[s][:, n, :], ident).then_inc(sem["xT_psum"], 1)

                def values_twice(s, w):
                    for b in range(2):
                        for half in range(2):
                            i = mm(misc[s][half * 64:half * 64 + 64, 1, 256 + b * P:256 + b * P + P],
                                   XT[s][:, b * 64:b * 64 + 64], w)
                    return i

                def scores(s, k, queries, keys, n, opened=False):
                    for b in range(2):
                        for c in range(2):
                            i = mm(wide[s][b * 64:b * 64 + 64, c, 0:n], queries[c * 64:c * 64 + 64, b * 64:b * 64 + 64],
                                   keys(c, b), start=not opened)
                    i.then_inc(sem["scores_psum"], 1)

                def transpose_probs(k, blocks):
                    for s in STREAMS:
                        pe.wait_ge(sem["probs_ready"], at("probs_ready", k, s))
                        flat = wide[s][:, :, :].rearrange("p a b -> p (a b)")
                        for j in range(blocks):
                            i = nc.tensor.transpose(flat[:, j * P:j * P + P], PR[s][:, j * P:j * P + P], ident)
                        i.then_inc(sem["probsT_psum"], 1)

                def attend(k, blocks, width, values):
                    for s in STREAMS:
                        pe.wait_ge(sem["probsT_ready"], at("probsT_ready", k, s))
                        for j in range(blocks):
                            for b in range(2):
                                h, v = values(s, j, b)
                                n = v.shape[1] * (width + 1)
                                i = mm(misc[s][b * 64:b * 64 + 64, 1, h * (width + 1):h * (width + 1) + n],
                                       PT[s][:, j, b * 64:b * 64 + 64], v.rearrange("p h d -> p (h d)"))
                        if k != 1:
                            i.then_inc(sem["heads_psum"], 1)

                def project(i, k, w):
                    for s in STREAMS:
                        pe.wait_ge(sem["heads_ready"], at("heads_ready", k, s))
                        nc.tensor.transpose(misc[s][:, 0, 0:P], OH[s][:, :], ident).then_inc(sem["headsT_psum"], 1)
                    for s in STREAMS:
                        pe.wait_ge(sem["headsT_ready"], at("headsT_ready", i, s))
                        mm(misc[s][:, 0, P:2 * P], OT[s][:, :], w).then_inc(sem["projected"], 1)

                for s in STREAMS:
                    pe.wait_ge(sem[f"ctx_loaded{s}"], (pair + 1) * CTX_LOADS)
                    nc.tensor.transpose(misc[s][:, 0, 0:P], CTX[s][:, 0:P], ident).then_inc(sem["ctxT_psum"], 1)
                pe.wait_ge(sem["x_loaded0"], (pair + 1) * 16)
                pe.wait_ge(sem["x_loaded1"], (pair + 1) * 16)
                pe.wait_ge(sem["ctxT_ready"], at("ctxT_ready", 0, 1))
                transpose_x(0, 0)

                for s in STREAMS:
                    pe.wait_ge(sem["xT_ready"], at("xT_ready", 0, s))
                    mm(misc[s][:, 1, 0:256], XT[s][:, :], wqkvoT[:, 0:2, :].rearrange("p a b -> p (a b)"))
                    values_twice(s, wqkvoT[:, 2, :]).then_inc(sem["qkv_psum"], 1)
                for s in STREAMS:
                    pe.wait_ge(sem["rope_done"], at("rope_done", 0, s))
                    pe.wait_ge(sem["v_ready"], at("v_ready", 0, s))
                    nc.tensor.transpose(misc[s][:, 0, 0:P], QK[s][:, 0:P], ident)
                    nc.tensor.transpose(misc[s][:, 1, 0:P], QK[s][:, P:2 * P], ident).then_inc(sem["qkT_psum"], 1)
                for s in STREAMS:
                    for c in range(2):
                        mm(wide[s][:, c, :], ident_b[:, :], causal_b[:, :].unsqueeze(1).broadcast_to([P, 8, 64]),
                           stop=False)
                    wait_apart(pe, ("qT_ready", at("qT_ready", 0, s)), ("kmask_ready", at("kmask_ready", 0, s)))
                    scores(s, 0, QT[s], lambda c, b: KM[s][c * 64:c * 64 + 64, :, b * 64:b * 64 + 64], 512, True)
                transpose_probs(0, 8)
                attend(0, 8, 8, lambda s, j, b: (2 * j, V1[s][:, b, 2 * j:2 * j + 2, :]))
                project(0, 0, wqkvoT[:, 3, :])

                transpose_x(1, 1)
                for s in STREAMS:
                    pe.wait_ge(sem["xT_ready"], at("xT_ready", 1, s))
                    for j in range(2):
                        mm(misc[s][:, 1 - j, j * P:j * P + P], wx[:, j, :], XT[s][:, :])
                    for b in range(2):
                        i = mm(misc[s][64:P, 1, 256 + b * P:256 + b * P + P], XT[s][:, b * 64:b * 64 + 64], wx[:, 2, :])
                    i.then_inc(sem["qkv_psum"], 1)
                for k in range(2):
                    for s in STREAMS:
                        if k == 0:
                            wait_apart(pe, ("qT_ready", at("qT_ready", 1, s)), ("kmask_ready", at("kmask_ready", 1, s)),
                                       ("ctx_prepared", at("ctx_prepared", 0, s)))
                        scores(s, 1 + k, QT[s], lambda c, b: KX[s][c * 64:c * 64 + 64, 4 * k:4 * k + 4, b, :, :]
                               .rearrange("p h a k -> p h (a k)"), 512)
                    transpose_probs(1 + k, 8)
                    if k == 0:
                        pe.wait_ge(sem["v_ready"], at("v_ready", 1, 1))
                    attend(1 + k, 8, 8, lambda s, j, b: (
                        (j // 4) * 8 + 4 * k + j % 4,
                        V2[s][:, b, (j // 4) * 8 + 4 * k + j % 4:(j // 4) * 8 + 4 * k + j % 4 + 1, :]))
                project(1, 1, wx[:, 3, :])

                def experts(k0, up_w, down_w, chunks, hidden):
                    def up(e):
                        for s in STREAMS:
                            for c in range(4):
                                i = mm(wide[s][:, e % 2, c * P:c * P + P], up_w[:, e, c * P:c * P + P], XT[s][:, :])
                            i.then_inc(sem["up_psum"], 1)

                    def down(e):
                        for s in STREAMS:
                            pe.wait_ge(sem[hidden], at(hidden, (k0 if hidden == "act_ready" else 0) + e, s))
                            if e >= 2:
                                pe.wait_ge(sem["expert_added"], at("expert_added", k0 + e - 2, s))
                            for c in range(chunks):
                                i = mm(misc[s][:, e % 2, 256:384], HT[s][:, e % 2, c, :], down_w[:, e, c, :],
                                       start=(c == 0), stop=(c == chunks - 1))
                            i.then_inc(sem["down_psum"], 1)

                    return up, down

                transpose_x(2, 2)
                for s in STREAMS:
                    pe.wait_ge(sem["xT_ready"], at("xT_ready", 2, s))
                    mm(misc[s][:, 1, 0:E], XT[s][:, :], router[:, :]).then_inc(sem["router_psum"], 1)
                pe.wait_ge(sem["expert_loaded"], 16 * 2 * E)
                up, down = experts(0, w13, w2, 2, "hidden_ready")
                up(0)
                for e in range(1, E):
                    up(e)
                    down(e - 1)
                down(E - 1)

                transpose_x(3, 3)
                for s in STREAMS:
                    pe.wait_ge(sem["xT_ready"], at("xT_ready", 3, s))
                    for c in range(4):
                        i = mm(misc[s][:, 1, c * P:c * P + P], win[:, c, :], XT[s][:, :])
                    i.then_inc(sem["in_psum"], 1)
                for s in STREAMS:
                    pe.wait_ge(sem["conv_silu"], at("conv_silu", 0, s))
                    for c in range(2):
                        mm(misc[s][0:DTR, 0, 128:256], wxp[:, c, 0:DTR], XS[s][:, c, :], start=(c == 0), stop=(c == 1))
                    for c in range(2):
                        i = mm(misc[s][0:32, 0, 256:384], wxp[:, c, DTR:96], XS[s][:, c, :], start=(c == 0),
                               stop=(c == 1))
                    i.then_inc(sem["xdbl_psum"], 1)
                for s in STREAMS:
                    pe.wait_ge(sem["dt_low_ready"], at("dt_low_ready", 0, s))
                    for c in range(2):
                        i = mm(misc[s][:, 1, c * P:c * P + P], wdt[:, c, :], DTL[s][:, :])
                    i.then_inc(sem["dt_psum"], 1)
                    pe.wait_ge(sem["k_squared"], at("k_squared", 0, s))
                    mm(misc[s][:, 0, 384:512], const("ones", DSTATE), KKS[s][0:DSTATE, :]).then_inc(sem["ksum_psum"], 1)
                pe.wait_ge(sem["kq_mid_copied"], at("kq_mid_copied", 0, 1))
                pe.wait_ge(sem["kq_split"], at("kq_split", 0, 1))
                for g in range(4):
                    for s in STREAMS:
                        if g:
                            pe.wait_ge(sem["kq_bc_ready"], at("kq_bc_ready", g - 1, s))
                        for kq in range(2):
                            for j in range(4):
                                n = 16 * kq + 4 * g + j
                                i = mm(wide[s][:, kq, j * P:j * P + P], select_b[:, n:n + 1].broadcast_to([96, P]), SPL[s][:, :])
                        i.then_inc(sem["kq_bc_psum"], 1)
                for s in STREAMS:
                    pe.wait_ge(sem["y_ready"], at("y_ready", 0, s))
                    for c in range(2):
                        i = mm(misc[s][:, 0, 0:P], Y[s][:, c, :], wout[:, c, :], start=(c == 0), stop=(c == 1))
                    i.then_inc(sem["ssm_projected"], 1)

                transpose_x(4, 4)
                for s in STREAMS:
                    for c in range(2):
                        mm(wide[s][:, c, 0:256], ident, PAD[s][:, :].unsqueeze(1).broadcast_to([P, 4, 64]), stop=False)
                    wait_apart(pe, ("xT_ready", at("xT_ready", 4, s)))
                    scores(s, 3, XT[s], lambda c, b: KC[s][c * 64:c * 64 + 64, :, b * 64:b * 64 + 64], 256, True)
                transpose_probs(3, 4)
                pe.wait_ge(sem["ctx_values_ready"], at("ctx_values_ready", 0, 1))
                attend(3, 4, 16, lambda s, j, b: (2 * j, V5[s][:, b, 2 * j:2 * j + 2, :]))

                transpose_x(5, 6)
                for s in STREAMS:
                    pe.wait_ge(sem["xT_ready"], at("xT_ready", 5, s))
                    for j in range(2):
                        mm(misc[s][:, 1 - j, j * P:j * P + P], wlast[:, j * P:j * P + P], XT[s][:, :])
                    values_twice(s, wlast[:, 2 * P:3 * P]).then_inc(sem["qkv_psum"], 1)
                for s in STREAMS:
                    wait_apart(pe, ("qT_ready", at("qT_ready", 2, s)), ("kmask_ready", at("kmask_ready", 2, s)))
                    scores(s, 4, QT[s], lambda c, b: KM[s][c * 64:c * 64 + 64, :, b * 64:b * 64 + 64], 512)
                transpose_probs(4, 8)
                pe.wait_ge(sem["v_ready"], at("v_ready", 2, 1))
                attend(4, 8, 8, lambda s, j, b: (2 * j, V1[s][:, b, 2 * j:2 * j + 2, :]))
                project(2, 3, wlproj[:, :])
                transpose_x(6, 7)
                for s in STREAMS:
                    pe.wait_ge(sem["xT_ready"], at("xT_ready", 6, s))
                    mm(misc[s][:, 1, 0:E], XT[s][:, :], gate_w[:, :]).then_inc(sem["router_psum"], 1)
                pe.wait_ge(sem["logits_read"], at("logits_read", 1, 1))
                pe.wait_ge(sem["late_loaded"], 16 * 2 * E)
                up, down = experts(E, w1, w2b, 4, "act_ready")
                up(0)
                for e in range(1, E):
                    up(e)
                    down(e - 1)
                down(E - 1)
                pe.wait_ge(sem["normed"], at("normed", 7, 1))


N_EARLY = 30

_INS = ["x", "ctx_2048", "mask_BxS2_ik0", "L0_attn_WQ_w", "L0_attn_WQ_b", "L0_attn_WK_w", "L0_attn_WK_b",
        "L0_attn_WV_w", "L0_attn_WV_b", "L0_attn_Wo_w", "L0_attn_Wo_b", "L0_xattn_w_qkv", "L0_xattn_w_proj",
        "L0_xattn_b_proj", "L0_ffn_moe_router", "L0_ffn_moe_w13", "L0_ffn_moe_w2", "L1_attn_in_proj_w",
        "L1_attn_conv_w", "L1_attn_conv_b", "L1_attn_x_proj_w", "L1_attn_dt_head_w", "L1_attn_dt_head_b",
        "L1_attn_out_proj_w", "L1_attn_D", "L1_xattn_b", "L1_ffn_ln1_w", "L1_ffn_ln1_b", "L1_ffn_w_qkv",
        "L1_ffn_w_proj", "L1_ffn_ln2_w", "L1_ffn_ln2_b", "L1_ffn_gate_w", "L1_ffn_gate_b", "L1_ffn_w1", "L1_ffn_w2"]


def constants(np):
    p = np.arange(P)
    c = np.zeros((P, N_CONST), np.float32)

    def put(name, v):
        c[:, CONST_AT[name]:CONST_AT[name] + CONST_COLS[name]] = v

    put("ident", np.eye(P))
    put("causal", np.where(np.arange(64)[None, :] <= (p % 64)[:, None], 0.0, NEG))
    freq = np.float32(1.0) / np.float32(10000.0) ** (np.float32(2.0) * np.arange(4, dtype=np.float32) / np.float32(8))
    angle = (p % 64).astype(np.float32)[:, None] * freq[None, :].astype(np.float32)
    put("cos", np.cos(angle))
    put("sin", np.sin(angle))
    put("nsin", -np.sin(angle))
    put("mask8", (p[:, None] % 64) // 8 == np.arange(8)[None, :])
    put("mask4", (p[:, None] % 64) // 16 == np.arange(4)[None, :])
    put("rank", np.tile(8.0 - np.arange(8), (P, 1)))
    put("select", (p[:, None] % 32) == np.arange(32)[None, :])
    put("ones", np.ones((P, P)))
    return c


def kernel(**inputs):
    import numpy as _np
    import concourse.bacc as _bacc
    from concourse import mybir as _mybir
    from concourse.bass_utils import run_bass_kernel_spmd as _run

    nc = _bacc.Bacc("TRN2", target_bir_lowering=False, num_devices=1)
    arrays, args = {}, {}
    for name in _INS:
        v = _np.ascontiguousarray(inputs[name])
        arrays[f"in_{name}_dram"] = v
        args[name] = nc.dram_tensor(f"in_{name}_dram", v.shape, _mybir.dt.from_np(v.dtype), kind="ExternalInput").ap()
    arrays["consts_dram"] = constants(_np)
    consts = nc.dram_tensor("consts_dram", (P, N_CONST), _mybir.dt.float32, kind="ExternalInput").ap()
    out = nc.dram_tensor("out_0_dram", (16, 64, 128), _mybir.dt.float32, kind="ExternalOutput").ap()
    post_norm_decoder(nc, args, consts, out)
    r = _run(nc, [arrays], core_ids=[0])
    return r.results[0]["out_0_dram"]
```

```python
from contextlib import ExitStack

import concourse.bass as bass
from concourse import mybir

ALU = mybir.AluOpType
ACT = mybir.ActivationFunctionType
AX = mybir.AxisListType
F32 = mybir.dt.float32
BF16 = mybir.dt.bfloat16
I32 = mybir.dt.int32

P = 128
EPS = 1e-5
DT_FLOOR = -80.0
NEG = -1e30
STREAMS = (0, 1)
DVE_STEPS = 63
DVE_BEGINNING_STEPS = 7
LAYER_NORMS = 8
CTX_LOADS = 7 * 16

PE_TURNS = ("010110110100111011010010000110000001000000001011011100100001101010101111111111101111011111"
            "010000110010110101000001010010000001010101000100101101101111110101010111")
ACT_TURNS = ("011010101011010101000010000100101000100110010101101101111111111101100001010100100100101010"
             "0100110110101011")
DVE_TURNS = ("011111010111111110010000000000000000000000100000000000000000011111110001011111111110001010"
             "110100100110111001110111111111010011110111111111010100001011011001010000000000110111110100"
             "111000011000111101011110000100001111110110100100000001111010111001001000111111")
POOL_TURNS = ("110110101010011001011010000101")

CONST_COLS = {"ident": 128, "causal": 64, "cos": 4, "sin": 4, "nsin": 4, "mask8": 8, "mask4": 4,
              "rank": 8, "select": 32, "ones": 128}
CONST_AT = {}
_at = 0
for _name, _n in CONST_COLS.items():
    CONST_AT[_name] = _at
    _at += _n
N_CONST = _at

PER_TILE = {
    "xT_psum": 7, "xT_ready": 7,
    "qkv_psum": 3, "rope_done": 1, "qkT_psum": 1, "qT_ready": 3, "kmask_ready": 3, "v_ready": 3,
    "ctxT_psum": 1, "ctxT_ready": 1, "ctx_used": 1, "ctx_values_ready": 1, "ctx_prepared": 1,
    "scores_psum": 5, "scores_shifted": 5, "probs_ready": 5, "probsT_psum": 5, "probsT_ready": 5,
    "heads_psum": 4, "heads_ready": 4, "headsT_psum": 3, "headsT_ready": 3, "projected": 3,
    "residual_biased": 3,
    "variance_ready": 8, "rstd_ready": 8, "normed": 8,
    "router_psum": 2, "top_diff": 1, "top_exp": 1, "logits_read": 2,
    "up_psum": 16, "act_ready": 16, "hidden_ready": 8, "down_psum": 16, "expert_added": 16,
    "in_psum": 1, "xpad_ready": 1, "conv_done": 1, "conv_silu": 1, "xdbl_psum": 1, "dt_low_ready": 1,
    "k_squared": 1, "dt_psum": 1, "dt_floored": 1, "dt_exp_ready": 1, "ksum_psum": 1, "kq_ready": 1, "kq_mid": 1, "kq_mid_copied": 1, "kq_split": 1,
    "k_bc_psum": 4, "k_bc_ready": 4, "q_bc_psum": 4, "q_bc_ready": 4, "xgain_ready": 1, "drive_ready": 2,
    "decay_raw": 2, "decay_ready": 2, "state_used": 2, "y_psum": 2, "y_ready": 1, "ssm_projected": 1,
}
PER_STREAM = ["x_loaded", "ctx_loaded", "out_stored", "result_free", "dve_step"]
ONCE = ["weights_loaded", "matrices_loaded", "expert_loaded", "late_loaded", "wT_psum", "wT_copied", "prepared_act", "prepared_dve",
        "prepared_pool", "cleared"]


def post_norm_decoder(nc, a, consts, out):
    B, S, D = a["x"].shape
    PAIRS = B * S // P // 2
    E = 8
    NH = 16
    DSTATE, DTR, DIN = 16, 64, 256

    with ExitStack() as ctx:
        def sb(name, shape, dt=F32):
            return ctx.enter_context(nc.sbuf_tensor(name, shape, dt))

        def two_semaphores(name):
            return [ctx.enter_context(nc.semaphore(f"{name}{s}")) for s in STREAMS]

        def two(name, shape, dt=F32):
            return [sb(f"{name}{s}", shape, dt) for s in STREAMS]

        sem = {n: ctx.enter_context(nc.semaphore(n)) for n in ONCE}
        sem.update((n, two_semaphores(n)) for n in [*PER_TILE, *PER_STREAM])

        wide = [ctx.enter_context(nc.psum_tensor(f"wide{s}", [P, 2, 512], F32)) for s in STREAMS]
        misc = [ctx.enter_context(nc.psum_tensor(f"misc{s}", [P, 2, 512], F32)) for s in STREAMS]

        cst = sb("cst", [P, N_CONST])
        ident_b = sb("ident_b", [P, P], BF16)
        causal_b = sb("causal_b", [P, 64], BF16)
        select_b = sb("select_b", [96, 32], BF16)
        wqkvoT = sb("wqkvoT", [P, 4, P])
        wx = sb("wx", [P, 4, P])
        win = sb("win", [P, 4, P])
        wxp = sb("wxp", [P, 2, 96])
        wdt = sb("wdt", [DTR, 2, P])
        wout = sb("wout", [P, 2, P])
        wlast = sb("wlast", [P, 3 * P])
        wlproj = sb("wlproj", [P, P])
        router = sb("router", [P, E])
        gate_w = sb("gate_w", [P, E])
        w13 = sb("w13", [P, E, 512])
        w2 = sb("w2", [P, E, 2, P])
        w1 = sb("w1", [P, E, 512])
        w2b = sb("w2b", [P, E, 4, P])
        b_qk = sb("b_qk", [P, 2 * P])
        b_v = sb("b_v", [P, P])
        b_o = sb("b_o", [P, 2, P])
        ln_w = sb("ln_w", [P, 2, P])
        ln_b = sb("ln_b", [P, 2, P])
        gate_b = sb("gate_b", [P, E])
        mask_b = sb("mask_b", [P, 1])
        conv_w = sb("conv_w", [P, 2, 4])
        conv_b = sb("conv_b", [P, 2])
        dt_b = sb("dt_b", [P, 2])
        skip_d = sb("skip_d", [P, 2])
        minus_half = sb("minus_half", [P, 1])

        X = two("X", [P, LAYER_NORMS + 1, P])
        XT = two("XT", [P, P])
        QK = two("QK", [P, 2 * P])
        QT = two("QT", [P, P])
        KC = two("KC", [P, 4, P])
        CTX = two("CTX", [P, 2 * P])
        CTXT = two("CTXT", [P, P])
        CV = two("CV", [P, 2, P])
        V1 = two("V1", [P, 2, NH, 9])
        V2 = two("V2", [P, 2, NH, 9])
        V5 = two("V5", [P, 2, 8, 17])
        PADI = two("PADI", [P, 64], I32)
        PAD = two("PAD", [P, 64])
        MX = two("MX", [P, NH])
        RC = two("RC", [P, NH])
        OH = two("OH", [P, P])
        OT = two("OT", [P, P])
        XB = two("XB", [P, P])
        R = two("R", [P, P])
        ST = two("ST", [P, 6])
        MV = two("MV", [P, 2])
        VE = two("VE", [P, 1])
        RS = two("RS", [P, 1])
        LG = two("LG", [P, 8, E])
        SM = two("SM", [P, 12])
        G = two("G", [P, E])
        XP = two("XP", [P, 2, 2, 67])
        XC = two("XC", [P, 2, P])
        XS = two("XS", [P, 2, P])
        ZS = two("ZS", [P, 2, P])
        DTL = two("DTL", [DTR, P])
        KKS = two("KKS", [32, P])
        RES = two("RES", [32, P])
        KQ = two("KQ", [32, P])
        KMID = two("KMID", [32, P], BF16)
        SPL = two("SPL", [96, P], BF16)
        TG = XC
        U = two("U", [P, 2, P])
        XU = two("XU", [P, 2, P])
        Y = two("Y", [P, 2, P])
        KB = two("KB", [P, DSTATE, P])
        KKB = two("KKB", [P, DSTATE, P])
        QB = two("QB", [P, DSTATE, P])
        DEC = two("DEC", [P, 2 * DSTATE, 64])
        DRV = two("DRV", [P, DSTATE, P])

        def part(buffers, first, last):
            return [t[:, first:last, :].rearrange("p a b -> p (a b)") for t in buffers]

        PR = part(KKB, 0, 8)
        PT = [t[:, 8:16, :] for t in KKB]
        KM = [t[:, 0:8, :] for t in DRV]
        KX = [t.rearrange("p (h b a k) -> p h b a k", h=8, b=2, a=2) for t in part(QB, 0, 16)]
        HT = [t.rearrange("p (e c t) -> p e c t", e=2, c=4) for t in part(KB, 0, 8)]
        ACTV = [t.rearrange("p (e f) -> p e f", e=2) for t in part(KB, 8, 12)]
        RA = part(KB, 12, 14)
        RB = part(KB, 14, 16)
        STATE = [DRV, KB]
        DECAY = [DEC, [t.rearrange("p n (b t) -> p (n b) t", b=2) for t in (KKB[0][:, :, :], KKB[1][:, :, :])]]

        def k_bank(s, g):
            return (wide[s][:, 0, :], misc[s][:, 1, :])[g % 2]

        raw = [t[:, j, :] for t in (KB[0], KB[1]) for j in range(16)]

        def const(name, parts=P):
            return cst[0:parts, CONST_AT[name]:CONST_AT[name] + CONST_COLS[name]]

        ident = const("ident")
        one_col = const("ones")[:, 0:1]
        mask8 = const("mask8").unsqueeze(2)
        mask4 = const("mask4").unsqueeze(2)

        def value(pair, ahead=0):
            def at(name, k, s=None):
                n = PER_TILE[name]
                return pair * n + (ahead * n + k + 1)
            return at

        def wait_apart(engine, s, *waits):
            waits = [(sem[name][s], engine.to_reg(value)) for name, value in waits]
            engine.wait_ge(sem["prepared_dve"], 1)
            for semaphore, value in waits:
                engine.wait_ge(semaphore, value)

        def in_turns(engine, tile, turns):
            def merge(streams, dropped=False):
                for turn in turns:
                    if next(streams[int(turn)], None) is None and not dropped:
                        raise AssertionError("more turns than steps")
                for stream in streams:
                    for _ in stream:
                        raise AssertionError("the turns don't cover all steps")

            def steps(*parts):
                for part in parts:
                    for _ in part():
                        yield True

            for _ in steps(tile(0, 0, 0)[0]):
                pass
            with engine.Fori(0, PAIRS - 1) as pair:
                merge([steps(tile(pair, 0, 0)[1], tile(pair, 1, 0)[0]), steps(*tile(pair + 1, -1, 1))])
            merge([steps(tile(PAIRS - 1, 0, 0)[1]), steps(*tile(PAIRS - 1, 0, 1))], dropped=True)

        x_tiles = a["x"].rearrange("(n c) s d -> n (c s) d", c=2)
        ctx_rows = a["ctx_2048"]
        ctx_tiles = ctx_rows.rearrange("(n c) s d -> n (c s) d", c=2)
        out_tiles = out.rearrange("(n c) s d -> n (c s) d", c=2)

        block = ctx.enter_context(nc.Block())

        @block.sync
        def _(sp):
            early_count = []

            def early(dst, src, slow=False):
                early_count.append(dst)
                sp.dma_start(dst, src, allow_slow_non_contiguous=slow).then_inc(sem["weights_loaded"], 16)

            def columns(name):
                return a[name].rearrange("(c p) -> p c", p=P)

            def load_tile(pair, s):
                n = pair * 2 + s
                sp.dma_start(X[s][:, 0, :], x_tiles[n]).then_inc(sem["x_loaded"][s], 16)
                sp.dma_start(CTX[s][:, :], ctx_tiles[n]).then_inc(sem["ctx_loaded"][s], 16)
                for b in range(2):
                    for half in range(2):
                        sp.dma_start(CV[s][half * 64:half * 64 + 64, b, :],
                                     ctx_rows[n * 2 + b][:, P:2 * P]).then_inc(sem["ctx_loaded"][s], 16)
                    sp.dma_start(PADI[s][b * 64:b * 64 + 64, :],
                                 a["mask_BxS2_ik0"][n * 2 + b].partition_broadcast(64)
                                 ).then_inc(sem["ctx_loaded"][s], 16)

            load_tile(0, 0)
            early(b_qk[:, 0:P], a["L0_attn_WQ_b"].partition_broadcast(P))
            early(b_qk[:, P:2 * P], a["L0_attn_WK_b"].partition_broadcast(P))
            early(b_v[:, :], a["L0_attn_WV_b"].partition_broadcast(P))
            early(b_o[:, 0, :], a["L0_attn_Wo_b"].partition_broadcast(P))
            early(b_o[:, 1, :], a["L0_xattn_b_proj"].partition_broadcast(P))
            early(ln_w[:, 0, :], a["L1_ffn_ln1_w"].partition_broadcast(P))
            early(ln_w[:, 1, :], a["L1_ffn_ln2_w"].partition_broadcast(P))
            early(ln_b[:, 0, :], a["L1_ffn_ln1_b"].partition_broadcast(P))
            early(ln_b[:, 1, :], a["L1_ffn_ln2_b"].partition_broadcast(P))
            early(gate_b[:, :], a["L1_ffn_gate_b"].partition_broadcast(P))
            early(mask_b[:, :], a["L1_xattn_b"].partition_broadcast(P))
            early(conv_w[:, :, :], a["L1_attn_conv_w"].rearrange("(c p) o k -> p c (o k)", p=P))
            early(conv_b[:, :], columns("L1_attn_conv_b"), slow=True)
            early(dt_b[:, :], columns("L1_attn_dt_head_b"), slow=True)
            early(skip_d[:, :], columns("L1_attn_D"), slow=True)
            assert len(early_count) == N_EARLY, len(early_count)
            load_tile(0, 1)
            for e in range(E):
                sp.dma_start(w13[:, e, :], a["L0_ffn_moe_w13"][e]).then_inc(sem["expert_loaded"], 16)
                sp.dma_start(w2[:, e, :, :], a["L0_ffn_moe_w2"][e].rearrange("(c p) d -> p c d", p=P)
                             ).then_inc(sem["expert_loaded"], 16)
            for e in range(E):
                sp.dma_start(w1[:, e, :], a["L1_ffn_w1"][e]).then_inc(sem["late_loaded"], 16)
                sp.dma_start(w2b[:, e, :, :], a["L1_ffn_w2"][e].rearrange("(c p) d -> p c d", p=P)
                             ).then_inc(sem["late_loaded"], 16)

            def store_tile(pair, s):
                at = value(pair)
                wait_apart(sp, s, ("normed", at("normed", 7)))
                sp.dma_start(out_tiles[pair * 2 + s], X[s][:, LAYER_NORMS, :]).then_inc(sem["out_stored"][s], 16)

            with sp.Fori(0, PAIRS - 1) as pair:
                at = value(pair)
                for s in STREAMS:
                    wait_apart(sp, s, ("normed", at("normed", 0)), ("ctx_used", at("ctx_used", 0)),
                               ("ctx_values_ready", at("ctx_values_ready", 0)))
                    load_tile(pair + 1, s)
                for s in STREAMS:
                    store_tile(pair, s)
                    wait_apart(sp, s, ("out_stored", (pair + 1) * 16))
                    sp.sem_inc(sem["result_free"][s], 1)
            for s in STREAMS:
                store_tile(PAIRS - 1, s)
                sp.wait_ge(sem["out_stored"][s], 16 * PAIRS)

        @block.gpsimd
        def _(pool):
            nc.gpsimd.memset(minus_half[:, :], -0.5).then_inc(sem["prepared_pool"], 1)
            pool.wait_ge(sem["prepared_pool"], 1)
            pool.wait_ge(sem["weights_loaded"], N_EARLY * 16)
            pool.wait_ge(sem["matrices_loaded"], N_MATRICES * 16)
            pool.wait_ge(sem["prepared_dve"], 1)

            def tile(pair, ahead, s):
                at = value(pair, ahead)

                def rstd(n):
                    pool.wait_ge(sem["variance_ready"][s], at("variance_ready", n, s))
                    nc.gpsimd.tensor_tensor(RS[s][:, :], VE[s][:, :], minus_half[:, :], ALU.pow
                                            ).then_inc(sem["rstd_ready"][s], 1)
                    yield

                def beginning():
                    pool.wait_ge(sem["x_loaded"][s], pair * 16 + (ahead * 16 + 16))
                    nc.gpsimd.tensor_tensor(XB[s][:, :], X[s][:, 0, :], b_o[:, 0, :], ALU.add
                                            ).then_inc(sem["residual_biased"][s], 1)
                    yield
                    pool.wait_ge(sem["ctx_loaded"][s], pair * CTX_LOADS + (ahead * CTX_LOADS + CTX_LOADS))
                    pool.wait_ge(sem["ctxT_ready"][s], at("ctxT_ready", 0, s))
                    keys = CTXT[s][:, :].rearrange("p (b k) -> p b k", b=2).unsqueeze(1)
                    nc.gpsimd.tensor_tensor(KX[s][:, :, :, 0, :], keys.broadcast_to([P, 8, 2, 64]),
                                            mask8.unsqueeze(3).broadcast_to([P, 8, 2, 64]), ALU.mult)
                    nc.gpsimd.tensor_tensor(KC[s][:, :, :], CTXT[s][:, :].unsqueeze(1).broadcast_to([P, 4, P]),
                                            mask4.broadcast_to([P, 4, P]), ALU.mult)
                    nc.gpsimd.tensor_copy(V2[s][0:64, :, :, 0:8],
                                          CV[s][0:64, :, :].rearrange("p b (h d) -> p b h d", d=8))
                    nc.gpsimd.tensor_scalar(PAD[s][:, :], PADI[s][:, :], -4 * NEG, 4 * NEG, ALU.mult, ALU.add
                                            ).then_inc(sem["ctx_used"][s], 1)
                    yield
                    wait_apart(pool, s, ("ctx_used", at("ctx_used", 0, s)))
                    nc.gpsimd.tensor_scalar(PAD[s][:, :], PAD[s][:, :], mask_b[:, 0:1], None, ALU.add
                                            ).then_inc(sem["ctx_prepared"][s], 1)
                    yield
                    yield from rstd(0)

                def rest():
                    pool.wait_ge(sem["normed"][s], at("normed", 0, s))
                    nc.gpsimd.tensor_tensor(XB[s][:, :], X[s][:, 1, :], b_o[:, 1, :], ALU.add
                                            ).then_inc(sem["residual_biased"][s], 1)
                    yield
                    yield from rstd(1)
                    yield from rstd(2)
                    for c in range(2):
                        if c == 0:
                            pool.wait_ge(sem["k_bc_ready"][s], at("k_bc_ready", 3, s))
                            pool.wait_ge(sem["xgain_ready"][s], at("xgain_ready", 0, s))
                        nc.gpsimd.tensor_tensor(STATE[c][s][:, :, :], KB[s][:, :, :],
                                                XU[s][:, c, :].unsqueeze(1).broadcast_to([P, DSTATE, P]),
                                                ALU.mult).then_inc(sem["drive_ready"][s], 1)
                        yield
                    for n in range(3, 7):
                        yield from rstd(n)
                    pool.wait_ge(sem["normed"][s], at("normed", 6, s))
                    nc.gpsimd.tensor_tensor(XB[s][:, :], R[s][:, :], X[s][:, 5, :], ALU.add
                                            ).then_inc(sem["residual_biased"][s], 1)
                    yield
                    yield from rstd(7)

                return beginning, rest

            in_turns(pool, tile, POOL_TURNS)

        @block.scalar
        def _(act):
            brought = []

            def bring(dst, src):
                brought.append(dst)
                act.dma_start(dst, src).then_inc(sem["matrices_loaded"], 16)

            bring(cst[:, :], consts)
            for j, n in enumerate(["WQ_w", "WK_w", "WV_w", "Wo_w"]):
                bring(raw[j], a["L0_attn_" + n])
            bring(KB[0][:, 4:7, :], a["L0_xattn_w_qkv"].rearrange("(c p) d -> p c d", p=P))
            bring(KB[0][:, 7, :], a["L0_xattn_w_proj"])
            bring(KB[0][:, 8:12, :], a["L1_attn_in_proj_w"].rearrange("(c p) d -> p c d", p=P))
            bring(KB[0][0:96, 12:14, :], a["L1_attn_x_proj_w"].rearrange("r (c d) -> r c d", c=2))
            bring(KB[0][:, 14:16, 0:DTR], a["L1_attn_dt_head_w"].rearrange("(c p) d -> p c d", p=P))
            bring(KB[1][:, 0:2, :], a["L1_attn_out_proj_w"].rearrange("r (c d) -> r c d", c=2))
            bring(router[:, :], a["L0_ffn_moe_router"])
            bring(gate_w[:, :], a["L1_ffn_gate_w"])
            bring(wlast[:, :], a["L1_ffn_w_qkv"])
            bring(wlproj[:, :], a["L1_ffn_w_proj"])
            assert len(brought) == N_MATRICES, len(brought)
            act.wait_ge(sem["matrices_loaded"], N_MATRICES * 16)
            nc.scalar.copy(ident_b[:, :], ident)
            nc.scalar.copy(causal_b[:, :], const("causal"))
            nc.scalar.copy(select_b[:, :], const("select", 96)).then_inc(sem["prepared_act"], 1)

            def tile(pair, ahead, s):
                at = value(pair, ahead)

                def x_transposed(i):
                    act.wait_ge(sem["xT_psum"][s], at("xT_psum", i, s))
                    nc.scalar.copy(XT[s][:, :], misc[s][:, 0, 0:P]).then_inc(sem["xT_ready"][s], 1)
                    yield

                def softmax(k, n, scale):
                    act.wait_ge(sem["scores_shifted"][s], at("scores_shifted", k, s))
                    nc.scalar.activation(PR[s][:, 0:n], PR[s][:, 0:n], ACT.Exp, scale=scale
                                         ).then_inc(sem["probs_ready"][s], 1)
                    yield
                    act.wait_ge(sem["probsT_psum"][s], at("probsT_psum", k, s))
                    nc.scalar.copy(PT[s][:, 0:n // P, :].rearrange("p a b -> p (a b)"),
                                   wide[s][:, :, :].rearrange("p a b -> p (a b)")[:, 0:n]
                                   ).then_inc(sem["probsT_ready"][s], 1)
                    yield

                def heads_transposed(i):
                    act.wait_ge(sem["headsT_psum"][s], at("headsT_psum", i, s))
                    nc.scalar.copy(OT[s][:, :], misc[s][:, 0, 0:P]).then_inc(sem["headsT_ready"][s], 1)
                    yield

                def beginning():
                    act.wait_ge(sem["prepared_dve"], 1)
                    act.wait_ge(sem["ctx_loaded"][s], pair * CTX_LOADS + (ahead * CTX_LOADS + CTX_LOADS))
                    act.wait_ge(sem["ctxT_psum"][s], at("ctxT_psum", 0, s))
                    nc.scalar.copy(CTXT[s][:, :], misc[s][:, 0, 0:P]).then_inc(sem["ctxT_ready"][s], 1)
                    for half in range(2):
                        rows = slice(half * 64, half * 64 + 64)
                        i = nc.scalar.copy(
                            V5[s][rows, :, half:8:2, 0:16],
                            CV[s][rows, :, :].rearrange("p b (h d) -> p b h d", d=16)[:, :, half:8:2, :])
                    i.then_inc(sem["ctx_values_ready"][s], 1)
                    yield
                    yield from x_transposed(0)
                    act.wait_ge(sem["qkT_psum"][s], at("qkT_psum", 0, s))
                    nc.scalar.copy(QT[s][:, :], misc[s][:, 0, 0:P]).then_inc(sem["qT_ready"][s], 1)
                    yield
                    yield from softmax(0, 1024, 8 ** -0.5)
                    yield from heads_transposed(0)

                def rest():
                    yield from x_transposed(1)
                    act.wait_ge(sem["qkv_psum"][s], at("qkv_psum", 1, s))
                    nc.scalar.copy(QT[s][:, :], misc[s][:, 1, 0:P]).then_inc(sem["qT_ready"][s], 1)
                    nc.scalar.copy(V2[s][64:P, :, :, 0:8],
                                   misc[s][64:P, 1, 256:512].rearrange("p (b h d) -> p b h d", b=2, d=8)
                                   ).then_inc(sem["v_ready"][s], 1)
                    yield
                    yield from softmax(1, 1024, 8 ** -0.5)
                    yield from softmax(2, 1024, 8 ** -0.5)
                    yield from heads_transposed(1)
                    yield from x_transposed(2)
                    act.wait_ge(sem["top_diff"][s], at("top_diff", 0, s))
                    nc.scalar.activation(SM[s][:, 5:6], SM[s][:, 4:5], ACT.Exp).then_inc(sem["top_exp"][s], 1)
                    yield
                    for e in range(E):
                        act.wait_ge(sem["up_psum"][s], at("up_psum", e, s))
                        nc.scalar.activation(ACTV[s][:, e % 2, :], wide[s][:, e % 2, 0:256], ACT.Silu
                                             ).then_inc(sem["act_ready"][s], 1)
                        yield
                    yield from x_transposed(3)
                    act.wait_ge(sem["in_psum"][s], at("in_psum", 0, s))
                    nc.scalar.copy(XP[s][:, :, :, 3:67].rearrange("p c b t -> p (c b) t"),
                                   misc[s][:, 1, 0:256].rearrange("p (c t) -> p c t", t=64)
                                   ).then_inc(sem["xpad_ready"][s], 1)
                    yield
                    nc.scalar.activation(ZS[s][:, :, :].rearrange("p c t -> p (c t)"), misc[s][:, 1, 256:512], ACT.Silu)
                    yield
                    act.wait_ge(sem["conv_done"][s], at("conv_done", 0, s))
                    nc.scalar.activation(XS[s][:, :, :], XC[s][:, :, :], ACT.Silu).then_inc(sem["conv_silu"][s], 1)
                    yield
                    act.wait_ge(sem["xdbl_psum"][s], at("xdbl_psum", 0, s))
                    nc.scalar.copy(DTL[s][:, :], misc[s][0:DTR, 0, 128:256]).then_inc(sem["dt_low_ready"][s], 1)
                    nc.scalar.copy(KQ[s][:, :], misc[s][0:32, 0, 256:384]).then_inc(sem["kq_ready"][s], 1)
                    nc.scalar.activation(KKS[s][:, :], misc[s][0:32, 0, 256:384], ACT.Square
                                         ).then_inc(sem["k_squared"][s], 1)
                    yield
                    act.wait_ge(sem["kq_mid"][s], at("kq_mid", 0, s))
                    nc.scalar.copy(SPL[s][32:64, :], KMID[s][:, :]).then_inc(sem["kq_mid_copied"][s], 1)
                    yield
                    act.wait_ge(sem["dt_floored"][s], at("dt_floored", 0, s))
                    nc.scalar.activation(TG[s][:, :, :], TG[s][:, :, :], ACT.Exp, scale=-1.0
                                         ).then_inc(sem["dt_exp_ready"][s], 1)
                    yield
                    for g in range(4):
                        act.wait_ge(sem["k_bc_psum"][s], at("k_bc_psum", g, s))
                        flat = lambda t: t[s][:, 4 * g:4 * g + 4, :].rearrange("p n t -> p (n t)")
                        nc.scalar.copy(flat(KB), k_bank(s, g))
                        nc.scalar.activation(flat(KKB), k_bank(s, g), ACT.Square).then_inc(sem["k_bc_ready"][s], 1)
                        yield
                    for c in range(2):
                        act.wait_ge(sem["decay_raw"][s], at("decay_raw", c, s))
                        nc.scalar.activation(DECAY[c][s][:, :, 1:64], DECAY[c][s][:, :, 1:64], ACT.Identity,
                                             bias=one_col, scale=-1.0).then_inc(sem["decay_ready"][s], 1)
                        yield
                    yield from x_transposed(4)
                    yield from softmax(3, 512, 0.25)
                    yield from x_transposed(5)
                    act.wait_ge(sem["qkv_psum"][s], at("qkv_psum", 2, s))
                    nc.scalar.copy(QT[s][:, :], misc[s][:, 1, 0:P]).then_inc(sem["qT_ready"][s], 1)
                    for half in range(2):
                        rows = slice(half * 64, half * 64 + 64)
                        i = nc.scalar.copy(
                            V1[s][rows, :, half:NH:2, 0:8],
                            misc[s][rows, 1, 256:512].rearrange("p (b h d) -> p b h d", b=2, d=8)[:, :, half:NH:2, :])
                    i.then_inc(sem["v_ready"][s], 1)
                    yield
                    yield from softmax(4, 1024, 8 ** -0.5)
                    yield from heads_transposed(2)
                    yield from x_transposed(6)
                    for e in range(E):
                        act.wait_ge(sem["up_psum"][s], at("up_psum", E + e, s))
                        nc.scalar.activation(HT[s][:, e % 2, :, :].rearrange("p c t -> p (c t)"), wide[s][:, e % 2, :],
                                             ACT.Gelu_apprx_tanh).then_inc(sem["act_ready"][s], 1)
                        yield

                return beginning, rest

            in_turns(act, tile, ACT_TURNS)

        @block.vector
        def _(dve):
            for s in STREAMS:
                for t in (V1, V2, V5, XP, DEC):
                    nc.vector.memset(t[s][:], 0.0).then_inc(sem["cleared"], 1)
            dve.wait_ge(sem["cleared"], 10)
            for s in STREAMS:
                nc.vector.memset(R[s][:, 0:1], 0.0).then_inc(sem["result_free"][s], 1)
            for s in STREAMS:
                nc.vector.memset(V1[s][0:64, :, 0:NH:2, 8:9], 1.0)
                nc.vector.memset(V1[s][64:P, :, 1:NH:2, 8:9], 1.0)
                nc.vector.memset(V2[s][:, :, :, 8:9], 1.0)
                nc.vector.memset(V5[s][0:64, :, 0:8:2, 16:17], 1.0)
                nc.vector.memset(V5[s][64:P, :, 1:8:2, 16:17], 1.0)
            dve.wait_ge(sem["matrices_loaded"], N_MATRICES * 16)
            for g, dst in enumerate([wqkvoT, wx, win]):
                dve.wait_ge(sem["wT_psum"], g + 1)
                nc.vector.tensor_copy(dst[:, :, :], wide[g % 2][:, 0, :].rearrange("p (a b) -> p a b", a=4)
                                      ).then_inc(sem["wT_copied"], 1)
            dve.wait_ge(sem["wT_psum"], 4)
            nc.vector.tensor_copy(wxp[:, :, :], misc[0][:, 0, 0:256].rearrange("p (a b) -> p a b", a=2)[:, :, 0:96])
            nc.vector.tensor_copy(wdt[:, :, :], misc[0][0:DTR, 0, 256:512].rearrange("p (a b) -> p a b", a=2))
            nc.vector.tensor_copy(wout[:, :, :], misc[0][:, 1, 0:256].rearrange("p (a b) -> p a b", a=2)
                                  ).then_inc(sem["wT_copied"], 1)
            dve.wait_ge(sem["weights_loaded"], N_EARLY * 16)
            nc.vector.tensor_scalar(mask_b[:, :], mask_b[:, :], 4.0, None, ALU.mult).then_inc(sem["prepared_dve"], 1)

            def tile(pair, ahead, s):
                at = value(pair, ahead)
                count = [0]
                last = [0]

                def step(instruction, s):
                    instruction.then_inc(sem["dve_step"][s], 1)
                    count[0] += 1
                    last[0] = count[0]

                def previous(s):
                    dve.wait_ge(sem["dve_step"][s], pair * DVE_STEPS + (ahead * DVE_STEPS + last[0]))

                def norm(n, source, affine=None, experts=None):
                    if experts is None:
                        previous(s)
                    else:
                        dve.wait_ge(sem["expert_added"][s], at("expert_added", experts, s))
                    step(nc.vector.bn_stats(ST[s][:, :], source(s)), s)
                    yield
                    wait_apart(dve, s, ("dve_step", pair * DVE_STEPS + (ahead * DVE_STEPS + last[0])))
                    step(nc.vector.bn_aggr(MV[s][:, :], ST[s][:, :]), s)
                    yield
                    previous(s)
                    nc.vector.tensor_scalar(VE[s][:, :], MV[s][:, 1:2], EPS, None, ALU.add
                                            ).then_inc(sem["variance_ready"][s], 1)
                    yield
                    dve.wait_ge(sem["rstd_ready"][s], at("rstd_ready", n, s))
                    i = nc.vector.tensor_scalar(X[s][:, n + 1, :], source(s), MV[s][:, 0:1], RS[s][:, 0:1],
                                                ALU.subtract, ALU.mult)
                    if affine is None:
                        i.then_inc(sem["normed"][s], 1)
                    else:
                        step(i, s)
                    yield
                    if affine is not None:
                        previous(s)
                        step(nc.vector.tensor_tensor(X[s][:, n + 1, :], X[s][:, n + 1, :], ln_w[:, affine, :],
                                                     ALU.mult), s)
                        yield
                        previous(s)
                        nc.vector.tensor_tensor(X[s][:, n + 1, :], X[s][:, n + 1, :], ln_b[:, affine, :],
                                                ALU.add).then_inc(sem["normed"][s], 1)
                        yield

                def shift(k, heads, keys):
                    n = heads * keys // 2
                    dve.wait_ge(sem["scores_psum"][s], at("scores_psum", k, s))
                    sc = wide[s][:, :, 0:n].rearrange("p a (h k) -> p a h k", k=keys)
                    step(nc.vector.tensor_reduce(MX[s][:, 0:heads].rearrange("p (a h) -> p a h", a=2), sc,
                                                 AX.X, ALU.max), s)
                    previous(s)
                    for half in range(2):
                        h = heads // 2
                        i = nc.vector.tensor_tensor(
                            PR[s][:, half * n:half * n + n].rearrange("p (h k) -> p h k", k=keys),
                            wide[s][:, half, 0:n].rearrange("p (h k) -> p h k", k=keys),
                            MX[s][:, half * h:half * h + h].unsqueeze(2).broadcast_to([P, h, keys]), ALU.subtract)
                    i.then_inc(sem["scores_shifted"][s], 1)
                    yield

                def heads_normed(i, heads, width):
                    dve.wait_ge(sem["heads_psum"][s], at("heads_psum", i, s))
                    o = misc[s][:, 1, 0:heads * (width + 1)].rearrange("p (h d) -> p h d", d=width + 1)
                    step(nc.vector.reciprocal(RC[s][:, 0:heads].unsqueeze(2), o[:, :, width:width + 1]), s)
                    yield
                    previous(s)
                    o = misc[s][:, 1, 0:heads * (width + 1)].rearrange("p (h d) -> p h d", d=width + 1)
                    nc.vector.tensor_tensor(OH[s][:, :].rearrange("p (h d) -> p h d", d=width), o[:, :, 0:width],
                                            RC[s][:, 0:heads].unsqueeze(2).broadcast_to([P, heads, width]),
                                            ALU.mult).then_inc(sem["heads_ready"][s], 1)
                    yield

                def mask_keys(i, source):
                    kt, ready, k = source
                    dve.wait_ge(sem[ready][s], at(ready, k, s))
                    nc.vector.tensor_tensor(KM[s], kt(s).unsqueeze(1).broadcast_to([P, 8, P]),
                                            mask8.broadcast_to([P, 8, P]), ALU.mult
                                            ).then_inc(sem["kmask_ready"][s], 1)
                    yield

                def best(logits, top, ranked, rank_max, hot, layer=None):
                    if layer is None:
                        previous(s)
                    else:
                        dve.wait_ge(sem["logits_read"][s], at("logits_read", layer, s))
                    step(nc.vector.tensor_reduce(SM[s][:, top:top + 1], LG[s][:, logits, :], AX.X, ALU.max), s)
                    yield
                    previous(s)
                    step(nc.vector.scalar_tensor_tensor(
                        out=LG[s][:, ranked, :], in0=LG[s][:, logits, :], scalar=SM[s][:, top:top + 1],
                        in1=const("rank"), op0=ALU.is_ge, op1=ALU.mult), s)
                    yield
                    previous(s)
                    step(nc.vector.tensor_reduce(SM[s][:, rank_max:rank_max + 1], LG[s][:, ranked, :], AX.X,
                                                 ALU.max), s)
                    yield
                    previous(s)
                    step(nc.vector.tensor_scalar(hot(s), LG[s][:, ranked, :], SM[s][:, rank_max:rank_max + 1],
                                                 None, ALU.is_equal), s)
                    yield

                def add_expert(k, e, before=None):
                    dve.wait_ge(sem["down_psum"][s], at("down_psum", k, s))
                    if e == 0:
                        previous(s)
                    else:
                        dve.wait_ge(sem["expert_added"][s], at("expert_added", k - 1, s))
                    nc.vector.scalar_tensor_tensor(
                        out=R[s][:, :], in0=misc[s][:, e % 2, 256:384], scalar=G[s][:, e:e + 1],
                        in1=(before(s) if before else R[s][:, :]), op0=ALU.mult, op1=ALU.add
                    ).then_inc(sem["expert_added"][s], 1)
                    yield

                def gated(e):
                    dve.wait_ge(sem["act_ready"][s], at("act_ready", e, s))
                    nc.vector.tensor_tensor(HT[s][:, e % 2, 0:2, :].rearrange("p c t -> p (c t)"),
                                            ACTV[s][:, e % 2, :], wide[s][:, e % 2, 256:512], ALU.mult
                                            ).then_inc(sem["hidden_ready"][s], 1)
                    yield

                def beginning():
                    dve.wait_ge(sem["qkv_psum"][s], at("qkv_psum", 0, s))
                    step(nc.vector.tensor_tensor(QK[s][:, :], misc[s][:, 1, 0:256], b_qk[:, :], ALU.add), s)
                    yield
                    previous(s)
                    pairs = lambda t: t[s][:, :].rearrange("p (h j d) -> p h j d", j=2, d=4)
                    wave = lambda n: const(n).unsqueeze(1).broadcast_to([P, 32, 4])
                    nc.vector.tensor_tensor(pairs(RA)[:, :, 0, :], pairs(QK)[:, :, 0, :], wave("cos"), ALU.mult)
                    nc.vector.tensor_tensor(pairs(RA)[:, :, 1, :], pairs(QK)[:, :, 1, :], wave("cos"), ALU.mult)
                    nc.vector.tensor_tensor(pairs(RB)[:, :, 0, :], pairs(QK)[:, :, 1, :], wave("nsin"), ALU.mult)
                    step(nc.vector.tensor_tensor(pairs(RB)[:, :, 1, :], pairs(QK)[:, :, 0, :], wave("sin"), ALU.mult), s)
                    yield
                    previous(s)
                    nc.vector.tensor_tensor(QK[s][:, :], RA[s][:, :], RB[s][:, :], ALU.add).then_inc(sem["rope_done"][s], 1)
                    yield
                    for half in range(2):
                        rows = slice(half * 64, half * 64 + 64)
                        split = lambda t: t.rearrange("p (h d) -> p h d", d=8)[:, half:NH:2, :]
                        for b in range(2):
                            i = nc.vector.tensor_tensor(V1[s][rows, b, half:NH:2, 0:8],
                                                        split(misc[s][rows, 1, 256 + b * P:256 + b * P + P]),
                                                        split(b_v[rows, :]), ALU.add)
                    i.then_inc(sem["v_ready"][s], 1)
                    yield
                    yield from mask_keys(0, (lambda s: misc[s][:, 1, 0:P], "qkT_psum", 0))
                    yield from shift(0, NH, 64)
                    yield from heads_normed(0, NH, 8)
                    dve.wait_ge(sem["projected"][s], at("projected", 0, s))
                    dve.wait_ge(sem["residual_biased"][s], at("residual_biased", 0, s))
                    step(nc.vector.tensor_tensor(R[s][:, :], misc[s][:, 0, P:2 * P], XB[s][:, :], ALU.add), s)
                    yield
                    yield from norm(0, lambda s: R[s][:, :])
                    assert count[0] == DVE_BEGINNING_STEPS, count[0]

                def rest():
                    count[0] = DVE_BEGINNING_STEPS
                    dve.wait_ge(sem["qkv_psum"][s], at("qkv_psum", 1, s))
                    dve.wait_ge(sem["ctx_prepared"][s], at("ctx_prepared", 0, s))
                    keys = misc[s][:, 0, P:2 * P].rearrange("p (b k) -> p b k", b=2).unsqueeze(1)
                    nc.vector.tensor_tensor(KX[s][:, :, :, 1, :], keys.broadcast_to([P, 8, 2, 64]),
                                            mask8.unsqueeze(3).broadcast_to([P, 8, 2, 64]), ALU.mult
                                            ).then_inc(sem["kmask_ready"][s], 1)
                    yield
                    yield from shift(1, 8, 128)
                    yield from shift(2, 8, 128)
                    yield from heads_normed(1, NH, 8)
                    dve.wait_ge(sem["projected"][s], at("projected", 1, s))
                    dve.wait_ge(sem["residual_biased"][s], at("residual_biased", 1, s))
                    step(nc.vector.tensor_tensor(R[s][:, :], misc[s][:, 0, P:2 * P], XB[s][:, :], ALU.add), s)
                    yield
                    yield from norm(1, lambda s: R[s][:, :])

                    dve.wait_ge(sem["router_psum"][s], at("router_psum", 0, s))
                    nc.vector.tensor_copy(LG[s][:, 0, :], misc[s][:, 1, 0:E]).then_inc(sem["logits_read"][s], 1)
                    yield
                    yield from best(0, 0, 1, 1, lambda s: LG[s][:, 2, :], 0)
                    previous(s)
                    step(nc.vector.scalar_tensor_tensor(out=LG[s][:, 3, :], in0=LG[s][:, 2, :], scalar=NEG,
                                                        in1=LG[s][:, 0, :], op0=ALU.mult, op1=ALU.add), s)
                    yield
                    yield from best(3, 2, 4, 3, lambda s: LG[s][:, 5, :])
                    nc.vector.tensor_tensor(SM[s][:, 4:5], SM[s][:, 2:3], SM[s][:, 0:1], ALU.subtract
                                            ).then_inc(sem["top_diff"][s], 1)
                    yield
                    dve.wait_ge(sem["top_exp"][s], at("top_exp", 0, s))
                    step(nc.vector.tensor_scalar(SM[s][:, 6:7], SM[s][:, 5:6], 1.0, None, ALU.add), s)
                    yield
                    previous(s)
                    step(nc.vector.reciprocal(SM[s][:, 7:8], SM[s][:, 6:7]), s)
                    yield
                    previous(s)
                    nc.vector.tensor_tensor(SM[s][:, 8:9], SM[s][:, 7:8], SM[s][:, 5:6], ALU.mult)
                    step(nc.vector.tensor_scalar(LG[s][:, 6, :], LG[s][:, 2, :], SM[s][:, 7:8], None, ALU.mult), s)
                    yield
                    previous(s)
                    step(nc.vector.scalar_tensor_tensor(out=G[s][:, :], in0=LG[s][:, 5, :], scalar=SM[s][:, 8:9],
                                                        in1=LG[s][:, 6, :], op0=ALU.mult, op1=ALU.add), s)
                    yield

                    yield from gated(0)
                    for e in range(1, E):
                        yield from gated(e)
                        yield from add_expert(e - 1, e - 1, (lambda s: X[s][:, 2, :]) if e == 1 else None)
                    yield from add_expert(E - 1, E - 1)
                    yield from norm(2, lambda s: R[s][:, :], experts=E - 1)

                    dve.wait_ge(sem["xpad_ready"][s], at("xpad_ready", 0, s))
                    for c in range(2):
                        i = nc.vector.tensor_scalar(XC[s][:, c, :].rearrange("p (b t) -> p b t", b=2),
                                                    XP[s][:, c, :, 0:64], conv_w[:, c, 0:1], conv_b[:, c:c + 1],
                                                    ALU.mult, ALU.add)
                    step(i, s)
                    yield
                    for j in range(1, 4):
                        previous(s)
                        for c in range(2):
                            xc = XC[s][:, c, :].rearrange("p (b t) -> p b t", b=2)
                            i = nc.vector.scalar_tensor_tensor(out=xc, in0=XP[s][:, c, :, j:j + 64],
                                                               scalar=conv_w[:, c, j:j + 1], in1=xc,
                                                               op0=ALU.mult, op1=ALU.add)
                        if j < 3:
                            step(i, s)
                        else:
                            i.then_inc(sem["conv_done"][s], 1)
                        yield
                    dve.wait_ge(sem["dt_psum"][s], at("dt_psum", 0, s))
                    for c in range(2):
                        i = nc.vector.tensor_scalar(TG[s][:, c, :], misc[s][:, 1, c * P:c * P + P], dt_b[:, c:c + 1],
                                                    DT_FLOOR, ALU.add, ALU.max)
                    i.then_inc(sem["dt_floored"][s], 1)
                    yield
                    dve.wait_ge(sem["kq_ready"][s], at("kq_ready", 0, s))
                    step(nc.vector.tensor_copy(SPL[s][0:32, :], KQ[s][:, :]), s)
                    yield
                    previous(s)
                    step(nc.vector.tensor_tensor(RES[s][:, :], KQ[s][:, :], SPL[s][0:32, :],
                                                 ALU.subtract), s)
                    yield
                    previous(s)
                    nc.vector.tensor_copy(KMID[s][:, :], RES[s][:, :]).then_inc(sem["kq_mid"][s], 1)
                    yield
                    dve.wait_ge(sem["kq_mid"][s], at("kq_mid", 0, s))
                    nc.vector.tensor_tensor(SPL[s][64:96, :], RES[s][:, :], KMID[s][:, :], ALU.subtract
                                            ).then_inc(sem["kq_split"][s], 1)
                    yield

                    def copy_q(g):
                        dve.wait_ge(sem["q_bc_psum"][s], at("q_bc_psum", g, s))
                        nc.vector.tensor_copy(QB[s][:, 4 * g:4 * g + 4, :].rearrange("p n t -> p (n t)"),
                                              wide[s][:, 1, :]).then_inc(sem["q_bc_ready"][s], 1)
                        yield

                    yield from copy_q(0)
                    dve.wait_ge(sem["dt_exp_ready"][s], at("dt_exp_ready", 0, s))
                    dve.wait_ge(sem["ksum_psum"][s], at("ksum_psum", 0, s))
                    step(nc.vector.scalar_tensor_tensor(
                        out=U[s][:, :, :], in0=TG[s][:, :, :], scalar=1.0,
                        in1=misc[s][:, 0, 384:512].unsqueeze(1).broadcast_to([P, 2, P]), op0=ALU.add, op1=ALU.add), s)
                    yield
                    previous(s)
                    step(nc.vector.reciprocal(U[s][:, :, :], U[s][:, :, :]), s)
                    yield
                    previous(s)
                    nc.vector.tensor_tensor(XU[s][:, :, :], XS[s][:, :, :], U[s][:, :, :], ALU.mult
                                            ).then_inc(sem["xgain_ready"][s], 1)
                    yield
                    for g in range(1, 4):
                        yield from copy_q(g)
                    for c in range(2):
                        if c == 0:
                            dve.wait_ge(sem["k_bc_ready"][s], at("k_bc_ready", 3, s))
                        else:
                            nc.vector.memset(DECAY[c][s][:, :, 0:1], 0.0)
                        rows = lambda t: t.rearrange("p n (b t) -> p n b t", b=2)[:, :, :, 1:64]
                        nc.vector.tensor_tensor(
                            DECAY[c][s][:, :, :].rearrange("p (n b) t -> p n b t", b=2)[:, :, :, 1:64],
                            rows(KKB[s][:, :, :]), rows(U[s][:, c:c + 1, :]).broadcast_to([P, DSTATE, 2, 63]),
                            ALU.mult).then_inc(sem["decay_raw"][s], 1)
                        yield
                    for c in range(2):
                        dve.wait_ge(sem["decay_ready"][s], at("decay_ready", c, s))
                        dve.wait_ge(sem["drive_ready"][s], at("drive_ready", c, s))
                        state = STATE[c][s][:, :, :].rearrange("p n t -> p (n t)")
                        step(nc.vector.tensor_tensor_scan(
                            state, DECAY[c][s][:, :, :].rearrange("p n t -> p (n t)"), state, 0.0,
                            ALU.mult, ALU.add), s)
                        yield
                        previous(s)
                        nc.vector.tensor_tensor(STATE[c][s][:, :, :], STATE[c][s][:, :, :], QB[s][:, :, :], ALU.mult
                                                ).then_inc(sem["state_used"][s], 1)
                        yield
                    dve.wait_ge(sem["y_psum"][s], at("y_psum", 1, s))
                    for c in range(2):
                        i = nc.vector.scalar_tensor_tensor(out=Y[s][:, c, :], in0=XS[s][:, c, :],
                                                           scalar=skip_d[:, c:c + 1], in1=misc[s][:, 1, c * P:c * P + P],
                                                           op0=ALU.mult, op1=ALU.add)
                    step(i, s)
                    yield
                    previous(s)
                    nc.vector.tensor_tensor(Y[s][:, :, :], Y[s][:, :, :], ZS[s][:, :, :], ALU.mult
                                            ).then_inc(sem["y_ready"][s], 1)
                    yield
                    dve.wait_ge(sem["ssm_projected"][s], at("ssm_projected", 0, s))
                    step(nc.vector.tensor_tensor(R[s][:, :], misc[s][:, 0, 0:P], X[s][:, 3, :], ALU.add), s)
                    yield
                    yield from norm(3, lambda s: R[s][:, :])

                    yield from shift(3, 8, 64)
                    yield from heads_normed(3 - 1, 8, 16)
                    dve.wait_ge(sem["heads_ready"][s], at("heads_ready", 2, s))
                    step(nc.vector.tensor_tensor(R[s][:, :], OH[s][:, :], X[s][:, 4, :], ALU.add), s)
                    yield
                    yield from norm(4, lambda s: R[s][:, :])

                    dve.wait_ge(sem["normed"][s], at("normed", 4, s))
                    yield from norm(5, lambda s: X[s][:, 5, :], affine=0)
                    yield from mask_keys(2, (lambda s: misc[s][:, 0, P:2 * P], "qkv_psum", 2))
                    yield from shift(4, NH, 64)
                    yield from heads_normed(3, NH, 8)
                    dve.wait_ge(sem["projected"][s], at("projected", 2, s))
                    step(nc.vector.tensor_tensor(R[s][:, :], misc[s][:, 0, P:2 * P], X[s][:, 5, :], ALU.add), s)
                    yield
                    yield from norm(6, lambda s: R[s][:, :], affine=1)
                    dve.wait_ge(sem["router_psum"][s], at("router_psum", 1, s))
                    nc.vector.tensor_tensor(LG[s][:, 0, :], misc[s][:, 1, 0:E], gate_b[:, :], ALU.add
                                            ).then_inc(sem["logits_read"][s], 1)
                    yield
                    yield from best(0, 0, 1, 1, lambda s: G[s][:, :], 1)
                    dve.wait_ge(sem["residual_biased"][s], at("residual_biased", 2, s))
                    for e in range(E):
                        yield from add_expert(E + e, e, (lambda s: XB[s][:, :]) if e == 0 else None)
                    dve.wait_ge(sem["result_free"][s], pair + (ahead + 1))
                    yield from norm(7, lambda s: R[s][:, :], experts=2 * E - 1)
                    assert count[0] == DVE_STEPS, count[0]

                return beginning, rest

            in_turns(dve, tile, DVE_TURNS)

        @block.tensor
        def _(pe):
            pe.wait_ge(sem["matrices_loaded"], N_MATRICES * 16)
            for g in range(3):
                if g == 2:
                    pe.wait_ge(sem["wT_copied"], 1)
                for j in range(4):
                    i = nc.tensor.transpose(wide[g % 2][:, 0, j * P:j * P + P], raw[4 * g + j], ident)
                i.then_inc(sem["wT_psum"], 1)
            for j in range(2):
                nc.tensor.transpose(misc[0][:, 0, j * P:j * P + 96], raw[12 + j][0:96, :], ident[0:96, 0:96])
                nc.tensor.transpose(misc[0][0:DTR, 0, 256 + j * P:256 + j * P + P], raw[14 + j][:, 0:DTR], ident)
                i = nc.tensor.transpose(misc[0][:, 1, j * P:j * P + P], raw[16 + j], ident)
            i.then_inc(sem["wT_psum"], 1)
            pe.wait_ge(sem["wT_copied"], 4)
            pe.wait_ge(sem["prepared_act"], 1)
            pe.wait_ge(sem["prepared_dve"], 1)

            def tile(pair, ahead, s):
                at = value(pair, ahead)

                def mm(out_, lhsT, rhs, start=True, stop=True):
                    return nc.tensor.matmul(out_, lhsT, rhs, start=start, stop=stop, skip_group_check=True)

                def transpose_x(i, n):
                    if n:
                        pe.wait_ge(sem["normed"][s], at("normed", n - 1, s))
                    nc.tensor.transpose(misc[s][:, 0, 0:P], X[s][:, n, :], ident).then_inc(sem["xT_psum"][s], 1)
                    yield

                def values_twice(s, w):
                    for b in range(2):
                        for half in range(2):
                            i = mm(misc[s][half * 64:half * 64 + 64, 1, 256 + b * P:256 + b * P + P],
                                   XT[s][:, b * 64:b * 64 + 64], w)
                    return i

                def scores(s, k, queries, keys, n, opened=False):
                    for b in range(2):
                        for c in range(2):
                            i = mm(wide[s][b * 64:b * 64 + 64, c, 0:n], queries[c * 64:c * 64 + 64, b * 64:b * 64 + 64],
                                   keys(c, b), start=not opened)
                    i.then_inc(sem["scores_psum"][s], 1)

                def transpose_probs(k, blocks):
                    pe.wait_ge(sem["probs_ready"][s], at("probs_ready", k, s))
                    flat = wide[s][:, :, :].rearrange("p a b -> p (a b)")
                    for j in range(blocks):
                        i = nc.tensor.transpose(flat[:, j * P:j * P + P], PR[s][:, j * P:j * P + P], ident)
                    i.then_inc(sem["probsT_psum"][s], 1)
                    yield

                def attend(k, blocks, width, values):
                    pe.wait_ge(sem["probsT_ready"][s], at("probsT_ready", k, s))
                    for j in range(blocks):
                        for b in range(2):
                            h, v = values(s, j, b)
                            n = v.shape[1] * (width + 1)
                            i = mm(misc[s][b * 64:b * 64 + 64, 1, h * (width + 1):h * (width + 1) + n],
                                   PT[s][:, j, b * 64:b * 64 + 64], v.rearrange("p h d -> p (h d)"))
                    if k != 1:
                        i.then_inc(sem["heads_psum"][s], 1)
                    yield

                def project(i, k, w):
                    pe.wait_ge(sem["heads_ready"][s], at("heads_ready", k, s))
                    nc.tensor.transpose(misc[s][:, 0, 0:P], OH[s][:, :], ident).then_inc(sem["headsT_psum"][s], 1)
                    yield
                    pe.wait_ge(sem["headsT_ready"][s], at("headsT_ready", i, s))
                    mm(misc[s][:, 0, P:2 * P], OT[s][:, :], w).then_inc(sem["projected"][s], 1)
                    yield

                def experts(k0, up_w, down_w, chunks, hidden):
                    def up(e):
                        for c in range(4):
                            i = mm(wide[s][:, e % 2, c * P:c * P + P], up_w[:, e, c * P:c * P + P], XT[s][:, :])
                        i.then_inc(sem["up_psum"][s], 1)
                        yield

                    def down(e):
                        pe.wait_ge(sem[hidden][s], at(hidden, (k0 if hidden == "act_ready" else 0) + e, s))
                        if e >= 2:
                            pe.wait_ge(sem["expert_added"][s], at("expert_added", k0 + e - 2, s))
                        for c in range(chunks):
                            i = mm(misc[s][:, e % 2, 256:384], HT[s][:, e % 2, c, :], down_w[:, e, c, :],
                                   start=(c == 0), stop=(c == chunks - 1))
                        i.then_inc(sem["down_psum"][s], 1)
                        yield

                    return up, down

                def beginning():
                    pe.wait_ge(sem["ctx_loaded"][s], pair * CTX_LOADS + (ahead * CTX_LOADS + CTX_LOADS))
                    nc.tensor.transpose(misc[s][:, 0, 0:P], CTX[s][:, 0:P], ident).then_inc(sem["ctxT_psum"][s], 1)
                    yield
                    pe.wait_ge(sem["x_loaded"][s], pair * 16 + (ahead * 16 + 16))
                    pe.wait_ge(sem["ctxT_ready"][s], at("ctxT_ready", 0, s))
                    yield from transpose_x(0, 0)

                    pe.wait_ge(sem["xT_ready"][s], at("xT_ready", 0, s))
                    mm(misc[s][:, 1, 0:256], XT[s][:, :], wqkvoT[:, 0:2, :].rearrange("p a b -> p (a b)"))
                    values_twice(s, wqkvoT[:, 2, :]).then_inc(sem["qkv_psum"][s], 1)
                    yield
                    pe.wait_ge(sem["rope_done"][s], at("rope_done", 0, s))
                    pe.wait_ge(sem["v_ready"][s], at("v_ready", 0, s))
                    nc.tensor.transpose(misc[s][:, 0, 0:P], QK[s][:, 0:P], ident)
                    nc.tensor.transpose(misc[s][:, 1, 0:P], QK[s][:, P:2 * P], ident).then_inc(sem["qkT_psum"][s], 1)
                    yield
                    for c in range(2):
                        mm(wide[s][:, c, :], ident_b[:, :], causal_b[:, :].unsqueeze(1).broadcast_to([P, 8, 64]),
                           stop=False)
                    wait_apart(pe, s, ("qT_ready", at("qT_ready", 0, s)), ("kmask_ready", at("kmask_ready", 0, s)))
                    scores(s, 0, QT[s], lambda c, b: KM[s][c * 64:c * 64 + 64, :, b * 64:b * 64 + 64], 512, True)
                    yield
                    yield from transpose_probs(0, 8)
                    yield from attend(0, 8, 8, lambda s, j, b: (2 * j, V1[s][:, b, 2 * j:2 * j + 2, :]))
                    yield from project(0, 0, wqkvoT[:, 3, :])

                def rest():
                    yield from transpose_x(1, 1)
                    pe.wait_ge(sem["xT_ready"][s], at("xT_ready", 1, s))
                    for j in range(2):
                        mm(misc[s][:, 1 - j, j * P:j * P + P], wx[:, j, :], XT[s][:, :])
                    for b in range(2):
                        i = mm(misc[s][64:P, 1, 256 + b * P:256 + b * P + P], XT[s][:, b * 64:b * 64 + 64], wx[:, 2, :])
                    i.then_inc(sem["qkv_psum"][s], 1)
                    yield
                    for k in range(2):
                        if k == 0:
                            wait_apart(pe, s, ("qT_ready", at("qT_ready", 1, s)), ("kmask_ready", at("kmask_ready", 1, s)),
                                       ("ctx_prepared", at("ctx_prepared", 0, s)))
                        scores(s, 1 + k, QT[s], lambda c, b: KX[s][c * 64:c * 64 + 64, 4 * k:4 * k + 4, b, :, :]
                               .rearrange("p h a k -> p h (a k)"), 512)
                        yield
                        yield from transpose_probs(1 + k, 8)
                        if k == 0:
                            pe.wait_ge(sem["v_ready"][s], at("v_ready", 1, s))
                        yield from attend(1 + k, 8, 8, lambda s, j, b: (
                            (j // 4) * 8 + 4 * k + j % 4,
                            V2[s][:, b, (j // 4) * 8 + 4 * k + j % 4:(j // 4) * 8 + 4 * k + j % 4 + 1, :]))
                    yield from project(1, 1, wx[:, 3, :])

                    yield from transpose_x(2, 2)
                    pe.wait_ge(sem["xT_ready"][s], at("xT_ready", 2, s))
                    mm(misc[s][:, 1, 0:E], XT[s][:, :], router[:, :]).then_inc(sem["router_psum"][s], 1)
                    yield
                    pe.wait_ge(sem["expert_loaded"], 16 * 2 * E)
                    up, down = experts(0, w13, w2, 2, "hidden_ready")
                    yield from up(0)
                    for e in range(1, E):
                        yield from up(e)
                        yield from down(e - 1)
                    yield from down(E - 1)

                    yield from transpose_x(3, 3)
                    pe.wait_ge(sem["xT_ready"][s], at("xT_ready", 3, s))
                    for c in range(4):
                        i = mm(misc[s][:, 1, c * P:c * P + P], win[:, c, :], XT[s][:, :])
                    i.then_inc(sem["in_psum"][s], 1)
                    yield
                    pe.wait_ge(sem["conv_silu"][s], at("conv_silu", 0, s))
                    for c in range(2):
                        mm(misc[s][0:DTR, 0, 128:256], wxp[:, c, 0:DTR], XS[s][:, c, :], start=(c == 0), stop=(c == 1))
                    for c in range(2):
                        i = mm(misc[s][0:32, 0, 256:384], wxp[:, c, DTR:96], XS[s][:, c, :], start=(c == 0),
                               stop=(c == 1))
                    i.then_inc(sem["xdbl_psum"][s], 1)
                    yield
                    pe.wait_ge(sem["dt_low_ready"][s], at("dt_low_ready", 0, s))
                    for c in range(2):
                        i = mm(misc[s][:, 1, c * P:c * P + P], wdt[:, c, :], DTL[s][:, :])
                    i.then_inc(sem["dt_psum"][s], 1)
                    pe.wait_ge(sem["k_squared"][s], at("k_squared", 0, s))
                    mm(misc[s][:, 0, 384:512], const("ones", DSTATE), KKS[s][0:DSTATE, :]).then_inc(sem["ksum_psum"][s], 1)
                    yield
                    pe.wait_ge(sem["kq_mid_copied"][s], at("kq_mid_copied", 0, s))
                    pe.wait_ge(sem["kq_split"][s], at("kq_split", 0, s))
                    for g in range(4):
                        if g >= 2:
                            pe.wait_ge(sem["k_bc_ready"][s], at("k_bc_ready", g - 2, s))
                        for j in range(4):
                            n = 4 * g + j
                            i = mm(k_bank(s, g)[:, j * P:j * P + P], select_b[:, n:n + 1].broadcast_to([96, P]),
                                   SPL[s][:, :])
                        i.then_inc(sem["k_bc_psum"][s], 1)
                        yield
                        if g:
                            pe.wait_ge(sem["q_bc_ready"][s], at("q_bc_ready", g - 1, s))
                        for j in range(4):
                            n = 16 + 4 * g + j
                            i = mm(wide[s][:, 1, j * P:j * P + P], select_b[:, n:n + 1].broadcast_to([96, P]),
                                   SPL[s][:, :])
                        i.then_inc(sem["q_bc_psum"][s], 1)
                        yield
                    for c in range(2):
                        pe.wait_ge(sem["state_used"][s], at("state_used", c, s))
                        for n in range(DSTATE):
                            i = mm(misc[s][:, 1, c * P:c * P + P], ident, STATE[c][s][:, n, :], start=(n == 0),
                                   stop=(n == DSTATE - 1))
                        i.then_inc(sem["y_psum"][s], 1)
                        yield
                    pe.wait_ge(sem["y_ready"][s], at("y_ready", 0, s))
                    for c in range(2):
                        i = mm(misc[s][:, 0, 0:P], Y[s][:, c, :], wout[:, c, :], start=(c == 0), stop=(c == 1))
                    i.then_inc(sem["ssm_projected"][s], 1)
                    yield

                    yield from transpose_x(4, 4)
                    for c in range(2):
                        mm(wide[s][:, c, 0:256], ident, PAD[s][:, :].unsqueeze(1).broadcast_to([P, 4, 64]), stop=False)
                    wait_apart(pe, s, ("xT_ready", at("xT_ready", 4, s)))
                    scores(s, 3, XT[s], lambda c, b: KC[s][c * 64:c * 64 + 64, :, b * 64:b * 64 + 64], 256, True)
                    yield
                    yield from transpose_probs(3, 4)
                    pe.wait_ge(sem["ctx_values_ready"][s], at("ctx_values_ready", 0, s))
                    yield from attend(3, 4, 16, lambda s, j, b: (2 * j, V5[s][:, b, 2 * j:2 * j + 2, :]))

                    yield from transpose_x(5, 6)
                    pe.wait_ge(sem["xT_ready"][s], at("xT_ready", 5, s))
                    for j in range(2):
                        mm(misc[s][:, 1 - j, j * P:j * P + P], wlast[:, j * P:j * P + P], XT[s][:, :])
                    values_twice(s, wlast[:, 2 * P:3 * P]).then_inc(sem["qkv_psum"][s], 1)
                    yield
                    wait_apart(pe, s, ("qT_ready", at("qT_ready", 2, s)), ("kmask_ready", at("kmask_ready", 2, s)))
                    scores(s, 4, QT[s], lambda c, b: KM[s][c * 64:c * 64 + 64, :, b * 64:b * 64 + 64], 512)
                    yield
                    yield from transpose_probs(4, 8)
                    pe.wait_ge(sem["v_ready"][s], at("v_ready", 2, s))
                    yield from attend(4, 8, 8, lambda s, j, b: (2 * j, V1[s][:, b, 2 * j:2 * j + 2, :]))
                    yield from project(2, 3, wlproj[:, :])
                    yield from transpose_x(6, 7)
                    pe.wait_ge(sem["xT_ready"][s], at("xT_ready", 6, s))
                    mm(misc[s][:, 1, 0:E], XT[s][:, :], gate_w[:, :]).then_inc(sem["router_psum"][s], 1)
                    yield
                    pe.wait_ge(sem["logits_read"][s], at("logits_read", 1, s))
                    pe.wait_ge(sem["late_loaded"], 16 * 2 * E)
                    up, down = experts(E, w1, w2b, 4, "act_ready")
                    yield from up(0)
                    for e in range(1, E):
                        yield from up(e)
                        yield from down(e - 1)
                    yield from down(E - 1)
                    pe.wait_ge(sem["expert_added"][s], at("expert_added", 2 * E - 1, s))

                return beginning, rest

            in_turns(pe, tile, PE_TURNS)


N_EARLY = 15
N_MATRICES = 15

_INS = ["x", "ctx_2048", "mask_BxS2_ik0", "L0_attn_WQ_w", "L0_attn_WQ_b", "L0_attn_WK_w", "L0_attn_WK_b",
        "L0_attn_WV_w", "L0_attn_WV_b", "L0_attn_Wo_w", "L0_attn_Wo_b", "L0_xattn_w_qkv", "L0_xattn_w_proj",
        "L0_xattn_b_proj", "L0_ffn_moe_router", "L0_ffn_moe_w13", "L0_ffn_moe_w2", "L1_attn_in_proj_w",
        "L1_attn_conv_w", "L1_attn_conv_b", "L1_attn_x_proj_w", "L1_attn_dt_head_w", "L1_attn_dt_head_b",
        "L1_attn_out_proj_w", "L1_attn_D", "L1_xattn_b", "L1_ffn_ln1_w", "L1_ffn_ln1_b", "L1_ffn_w_qkv",
        "L1_ffn_w_proj", "L1_ffn_ln2_w", "L1_ffn_ln2_b", "L1_ffn_gate_w", "L1_ffn_gate_b", "L1_ffn_w1", "L1_ffn_w2"]


def constants(np):
    p = np.arange(P)
    c = np.zeros((P, N_CONST), np.float32)

    def put(name, v):
        c[:, CONST_AT[name]:CONST_AT[name] + CONST_COLS[name]] = v

    put("ident", np.eye(P))
    put("causal", np.where(np.arange(64)[None, :] <= (p % 64)[:, None], 0.0, NEG))
    freq = np.float32(1.0) / np.float32(10000.0) ** (np.float32(2.0) * np.arange(4, dtype=np.float32) / np.float32(8))
    angle = (p % 64).astype(np.float32)[:, None] * freq[None, :].astype(np.float32)
    put("cos", np.cos(angle))
    put("sin", np.sin(angle))
    put("nsin", -np.sin(angle))
    put("mask8", (p[:, None] % 64) // 8 == np.arange(8)[None, :])
    put("mask4", (p[:, None] % 64) // 16 == np.arange(4)[None, :])
    put("rank", np.tile(8.0 - np.arange(8), (P, 1)))
    put("select", (p[:, None] % 32) == np.arange(32)[None, :])
    put("ones", np.ones((P, P)))
    return c


def kernel(**inputs):
    import numpy as _np
    import concourse.bacc as _bacc
    from concourse import mybir as _mybir
    from concourse.bass_utils import run_bass_kernel_spmd as _run

    nc = _bacc.Bacc("TRN2", target_bir_lowering=False, num_devices=1)
    arrays, args = {}, {}
    for name in _INS:
        v = _np.ascontiguousarray(inputs[name])
        arrays[f"in_{name}_dram"] = v
        args[name] = nc.dram_tensor(f"in_{name}_dram", v.shape, _mybir.dt.from_np(v.dtype), kind="ExternalInput").ap()
    arrays["consts_dram"] = constants(_np)
    consts = nc.dram_tensor("consts_dram", (P, N_CONST), _mybir.dt.float32, kind="ExternalInput").ap()
    out = nc.dram_tensor("out_0_dram", (16, 64, 128), _mybir.dt.float32, kind="ExternalOutput").ap()
    post_norm_decoder(nc, args, consts, out)
    r = _run(nc, [arrays], core_ids=[0])
    return r.results[0]["out_0_dram"]
```
